# Optimizing a Trainium2 kernel written in Bass

```python
import numpy as np
import jax
import jax.numpy as jnp

def _softmax(x, axis=-1):
    return jax.nn.softmax(x, axis=axis)

def _gelu(x):
    return jax.nn.gelu(x, approximate=True)

def _silu(x):
    return jax.nn.silu(x)

def _sigmoid(x):
    return jax.nn.sigmoid(x)

def _layernorm(x, axis=-1, eps=1e-05):
    m = jnp.mean(x, axis=axis, keepdims=True)
    v = jnp.var(x, axis=axis, keepdims=True)
    return (x - m) / jnp.sqrt(v + eps)

def _scatter_add(tgt, idx, src, axis=0):
    return tgt.at[idx].add(src)

def _segment_sum(src, seg, n):
    return jax.ops.segment_sum(src, seg, n)
kernel_name = 'mk_recurrent_d1_jaxref_r8_36ad3b'

def setup_inputs(seed: int=0):
    np.random.seed(seed)
    _w = jnp.asarray

    def _L0_attn_setup():
        import jax, jax.numpy as jnp
        import numpy as np
        ROPE_DIM = 64
        GN_GROUPS = 32
        GN_CHANNELS = 256
        GN_EPS = 1e-05

        def rope_rotate(x):
            T = x.shape[-2]
            inv_freq = 1.0 / 10000.0 ** (jnp.arange(0, ROPE_DIM, 2, dtype=jnp.float32) / ROPE_DIM)
            freqs = jnp.arange(T, dtype=jnp.float32)[:, None] * inv_freq[None, :]
            freqs = jnp.repeat(freqs, 2, axis=-1)
            cos, sin = (jnp.cos(freqs), jnp.sin(freqs))
            xr = x[..., :ROPE_DIM]
            x1, x2 = (xr[..., 0::2], xr[..., 1::2])
            rot = jnp.stack((-x2, x1), axis=-1).reshape(xr.shape)
            xr = xr * cos + rot * sin
            return jnp.concatenate([xr, x[..., ROPE_DIM:]], axis=-1)

        def group_norm_rows(x2d, weight, bias):
            N, Cc = x2d.shape
            xg = x2d.reshape(N, GN_GROUPS, Cc // GN_GROUPS)
            mu = xg.mean(-1, keepdims=True)
            var = xg.var(-1, keepdims=True)
            xn = ((xg - mu) * jax.lax.rsqrt(var + GN_EPS)).reshape(N, Cc)
            return xn * weight + bias

        def _reference_tuple_inner(X, S_n, W_Q, hh_b, gn_weight, gn_bias):
            B, T, _ = X.shape
            Q = jax.nn.relu(rope_rotate(X @ W_Q))
            H = jnp.tanh(Q + hh_b)
            C = H.shape[-1]
            out = group_norm_rows(H.reshape(-1, C), gn_weight, gn_bias).reshape(B, T, C)
            out = jnp.swapaxes(out, -2, -1).reshape(B, T, C)
            return (out, S_n)
        key = jax.random.key(seed)
        ks = jax.random.split(key, 4)
        B, T, I, C = (2, 512, 256, 256)
        X = jax.random.normal(ks[0], (B, T, I), dtype=jnp.float32)
        S_n = jnp.zeros((B, C), dtype=jnp.float32)
        W_Q = jax.random.normal(ks[1], (I, C), dtype=jnp.float32) / I
        hh_b = jax.random.normal(ks[2], (C,), dtype=jnp.float32) * 0.02
        gn_weight = jnp.ones((C,), dtype=jnp.float32)
        gn_bias = jnp.zeros((C,), dtype=jnp.float32)
        return {'X': X, 'S_n': S_n, 'W_Q': W_Q, 'hh_b': hh_b, 'gn_weight': gn_weight, 'gn_bias': gn_bias}
    _L0_attn_in = _L0_attn_setup()

    def _L0_ffn_setup():
        import jax, jax.numpy as jnp
        import numpy as np
        D = 256
        M = 128
        E = 32
        K = 6
        G = 8
        KG = 4
        SH = 256
        SCALE = 2.5

        def _route(xf, Wr, br):
            T = xf.shape[0]
            s = jax.nn.sigmoid(xf @ Wr.T + br)
            sg = s.reshape(T, G, E // G)
            group_w = jax.lax.top_k(sg, 2)[0].sum(-1)
            top_g = jax.lax.top_k(group_w, KG)[1]
            gmask = jnp.zeros((T, G), bool).at[jnp.arange(T)[:, None], top_g].set(True)
            masked = jnp.where(gmask[:, :, None], sg, 0.0).reshape(T, E)
            idx = jax.lax.top_k(masked, K)[1]
            w = jnp.take_along_axis(s, idx, axis=1)
            w = w / (w.sum(-1, keepdims=True) + 1e-20)
            return (idx, w * SCALE)
        key = jax.random.key(seed)
        ks = jax.random.split(key, 7)
        w = 0.02
        return {'hidden_tensor': jax.random.normal(ks[0], (2, 256, D), dtype=jnp.float32), 'Wr': jax.random.normal(ks[1], (E, D), dtype=jnp.float32) * w, 'br': jax.random.normal(ks[2], (E,), dtype=jnp.float32) * w, 'W1': jax.random.normal(ks[3], (E, M, D), dtype=jnp.float32) * w, 'W2': jax.random.normal(ks[4], (E, D, M), dtype=jnp.float32) * w, 'Ws1': jax.random.normal(ks[5], (SH, D), dtype=jnp.float32) * w, 'Ws2': jax.random.normal(ks[6], (D, SH), dtype=jnp.float32) * w}
    _L0_ffn_in = _L0_ffn_setup()
    _d = {'L0_attn_X': _L0_attn_in['X'], 'L0_attn_S_n': _L0_attn_in['S_n'], 'L0_attn_W_Q': _L0_attn_in['W_Q'], 'L0_attn_hh_b': _L0_attn_in['hh_b'], 'L0_attn_gn_weight': _L0_attn_in['gn_weight'], 'L0_attn_gn_bias': _L0_attn_in['gn_bias'], 'L0_ffn_Wr': _L0_ffn_in['Wr'], 'L0_ffn_br': _L0_ffn_in['br'], 'L0_ffn_W1': _L0_ffn_in['W1'], 'L0_ffn_W2': _L0_ffn_in['W2'], 'L0_ffn_Ws1': _L0_ffn_in['Ws1'], 'L0_ffn_Ws2': _L0_ffn_in['Ws2']}
    _x0 = _d['L0_attn_X']
    _d['L0_attn_X'] = jax.random.normal(jax.random.fold_in(jax.random.key(seed), 1), (2, 1024, 256), dtype=_x0.dtype)
    del _x0
    return _d

def reference(L0_attn_X, L0_attn_S_n, L0_attn_W_Q, L0_attn_hh_b, L0_attn_gn_weight, L0_attn_gn_bias, L0_ffn_Wr, L0_ffn_br, L0_ffn_W1, L0_ffn_W2, L0_ffn_Ws1, L0_ffn_Ws2):

    def _L0_attn_ref(X, S_n, W_Q, hh_b, gn_weight, gn_bias):
        import jax, jax.numpy as jnp
        import numpy as np
        ROPE_DIM = 64
        GN_GROUPS = 32
        GN_CHANNELS = 256
        GN_EPS = 1e-05

        def rope_rotate(x):
            T = x.shape[-2]
            inv_freq = 1.0 / 10000.0 ** (jnp.arange(0, ROPE_DIM, 2, dtype=jnp.float32) / ROPE_DIM)
            freqs = jnp.arange(T, dtype=jnp.float32)[:, None] * inv_freq[None, :]
            freqs = jnp.repeat(freqs, 2, axis=-1)
            cos, sin = (jnp.cos(freqs), jnp.sin(freqs))
            xr = x[..., :ROPE_DIM]
            x1, x2 = (xr[..., 0::2], xr[..., 1::2])
            rot = jnp.stack((-x2, x1), axis=-1).reshape(xr.shape)
            xr = xr * cos + rot * sin
            return jnp.concatenate([xr, x[..., ROPE_DIM:]], axis=-1)

        def group_norm_rows(x2d, weight, bias):
            N, Cc = x2d.shape
            xg = x2d.reshape(N, GN_GROUPS, Cc // GN_GROUPS)
            mu = xg.mean(-1, keepdims=True)
            var = xg.var(-1, keepdims=True)
            xn = ((xg - mu) * jax.lax.rsqrt(var + GN_EPS)).reshape(N, Cc)
            return xn * weight + bias

        def _reference_tuple_inner(X, S_n, W_Q, hh_b, gn_weight, gn_bias):
            B, T, _ = X.shape
            Q = jax.nn.relu(rope_rotate(X @ W_Q))
            H = jnp.tanh(Q + hh_b)
            C = H.shape[-1]
            out = group_norm_rows(H.reshape(-1, C), gn_weight, gn_bias).reshape(B, T, C)
            out = jnp.swapaxes(out, -2, -1).reshape(B, T, C)
            return (out, S_n)
        return _reference_tuple_inner(X, S_n, W_Q, hh_b, gn_weight, gn_bias)[0]

    def _L0_ffn_ref(hidden_tensor, Wr, br, W1, W2, Ws1, Ws2):
        import jax, jax.numpy as jnp
        import numpy as np
        D = 256
        M = 128
        E = 32
        K = 6
        G = 8
        KG = 4
        SH = 256
        SCALE = 2.5

        def _route(xf, Wr, br):
            T = xf.shape[0]
            s = jax.nn.sigmoid(xf @ Wr.T + br)
            sg = s.reshape(T, G, E // G)
            group_w = jax.lax.top_k(sg, 2)[0].sum(-1)
            top_g = jax.lax.top_k(group_w, KG)[1]
            gmask = jnp.zeros((T, G), bool).at[jnp.arange(T)[:, None], top_g].set(True)
            masked = jnp.where(gmask[:, :, None], sg, 0.0).reshape(T, E)
            idx = jax.lax.top_k(masked, K)[1]
            w = jnp.take_along_axis(s, idx, axis=1)
            w = w / (w.sum(-1, keepdims=True) + 1e-20)
            return (idx, w * SCALE)
        B, Tlen, C = hidden_tensor.shape
        xf = hidden_tensor.reshape(-1, C).astype(jnp.float32)
        T = xf.shape[0]
        idx, w = _route(xf, Wr, br)
        gate = jnp.zeros((T, E), w.dtype).at[jnp.arange(T)[:, None], idx].add(w)

        def step(acc, ew):
            w1, w2, g = ew
            h = jnp.square(jax.nn.relu(xf @ w1.T)) @ w2.T
            return (acc + g[:, None] * h, None)
        acc, _ = jax.lax.scan(step, jnp.zeros_like(xf), (W1, W2, gate.T))
        moe_out = acc.reshape(B, Tlen, C).astype(hidden_tensor.dtype)
        shared = jnp.square(jax.nn.relu(hidden_tensor @ Ws1.T)) @ Ws2.T
        return shared + moe_out
    x = L0_attn_X
    xn = _layernorm(x, axis=-1)
    s = _L0_attn_ref(xn, L0_attn_S_n, L0_attn_W_Q, L0_attn_hh_b, L0_attn_gn_weight, L0_attn_gn_bias)
    g = _silu(_L0_ffn_ref(xn, L0_ffn_Wr, L0_ffn_br, L0_ffn_W1, L0_ffn_W2, L0_ffn_Ws1, L0_ffn_Ws2))
    x = x + s * g
    return x

_drawn_inputs = setup_inputs


def setup_inputs(seed=0):
    import zlib

    import numpy as np

    out = dict(_drawn_inputs(seed))
    spreads = {'L0_attn_S_n': (0.0, 0.1), 'L0_attn_gn_weight': (1.0, 0.6), 'L0_attn_gn_bias': (0.0, 0.8)}
    factors = {'L0_attn_hh_b': 3.891,
     'L0_ffn_Wr': 4.16,
     'L0_ffn_br': 8.0,
     'L0_ffn_W1': 4.098,
     'L0_ffn_W2': 3.728,
     'L0_ffn_Ws1': 2.942,
     'L0_ffn_Ws2': 2.667}
    for name, (base, spread) in spreads.items():
        noise = np.random.default_rng([zlib.crc32(name.encode()), seed]).standard_normal(out[name].shape)
        drawn = base * np.exp(spread * noise) if base else spread * noise
        out[name] = jnp.asarray(drawn.astype(out[name].dtype))
    for name, factor in factors.items():
        out[name] = (out[name] * factor).astype(out[name].dtype)
    return out
```

```python
import numpy as np
import concourse.bass as bass
from concourse import mybir
from contextlib import ExitStack

ALU = mybir.AluOpType
ACT = mybir.ActivationFunctionType
AX = mybir.AxisListType
F32 = mybir.dt.float32
F16 = mybir.dt.float16

P = 128
B, T, D = 2, 1024, 256
KC = D // P
E, M = 32, 128
SH = 256
NS = SH // M
N = NS + E
G, EG = 8, E // 8
KG, K = 4, 6
CH = 512
NCH = B * T // CH
J = CH // P
NT = B * T // P
NG, GW = 32, 8
ROPE = 64
WCOLS = D + D
RING = 4
LAG = 3
GROUP = 2

W_SCALE = 64.0
WQ_SCALE = 256.0
SCALE = 2.5
MARK = 4.0
NONE = -1.0


def build(nc, x, wts, wr, br, wq, hh_b, gn_w, gn_b, cos, sin, ident, out, gates):
    with ExitStack() as ctx:
        def sb(name, shape, dt=F32):
            return ctx.enter_context(nc.sbuf_tensor(name, shape, dt))

        def sem(name):
            return ctx.enter_context(nc.semaphore(name))

        xs = sb("xs", [P, NCH, J, D])
        xhi = sb("xhi", [P, KC, B * T], F16)
        xlo = sb("xlo", [P, KC, B * T], F16)
        whi = sb("whi", [P, N * WCOLS], F16)
        wlo = sb("wlo", [P, N * WCOLS], F16)
        hn = sb("hn", [P, B, J, KC, D])
        wr_sb = sb("wr_sb", [P, KC, E])
        br_sb = sb("br_sb", [P, E])
        wq_sb = sb("wq_sb", [P, KC, D])
        wqhi = sb("wqhi", [P, KC, D], F16)
        wqlo = sb("wqlo", [P, KC, D], F16)
        hb_sb = sb("hb_sb", [P, D])
        hbs = sb("hbs", [P, D])
        gw_sb = sb("gw_sb", [P, D])
        gb_sb = sb("gb_sb", [P, D])
        cos_sb = sb("cos_sb", [P, T // P, ROPE])
        sin_sb = sb("sin_sb", [P, T // P, ROPE])
        id_sb = sb("id_sb", [P, P])
        power = sb("power", [P, NG * 2])
        wst = sb("wst", [P, RING, GROUP * WCOLS])
        gate_bc = sb("gate_bc", [P, RING, CH])
        relu = sb("relu", [P, RING, CH])
        hhi = sb("hhi", [P, RING, CH], F16)
        hlo = sb("hlo", [P, RING, CH], F16)
        xn = sb("xn", [P, J, D])
        xf = sb("xf", [P, KC, CH])
        stats = sb("stats", [P, J, 6])
        mv = sb("mv", [P, J, 2])
        vare = sb("vare", [P, J])
        rstd = sb("rstd", [P, J])
        zs = sb("zs", [P, J, E])
        th = sb("th", [P, J, E])
        ss = sb("ss", [P, J, E])
        pairs = sb("pairs", [P, J * G, 6])
        gsum = sb("gsum", [P, J, 2 * G])
        top_g = sb("top_g", [P, J, 8])
        gmark = sb("gmark", [P, J, 2 * G])
        gmask = sb("gmask", [P, J, G])
        masked = sb("masked", [P, J, E + 8])
        top_e = sb("top_e", [P, J, 8])
        emark = sb("emark", [P, J, E + 8])
        sel = sb("sel", [P, J, E])
        wsum = sb("wsum", [P, J])
        wrec = sb("wrec", [P, J])
        gate = sb("gate", [P, E, J])
        gate_t = sb("gate_t", [P, P])
        ra = sb("ra", [P, 2, ROPE])
        rb = sb("rb", [P, 2, ROPE])
        hpre = sb("hpre", [P, 2, D])
        hh = sb("hh", [P, 2, D])
        hd = sb("hd", [P, 2, D])
        hsq = sb("hsq", [P, 2, D])
        hnorm = sb("hnorm", [P, 2, D])
        hgain = sb("hgain", [P, 2, D])
        gmean = sb("gmean", [P, 2 * NG])
        gvar = sb("gvar", [P, 2 * NG])
        gvare = sb("gvare", [P, 2 * NG])
        grstd = sb("grstd", [P, 2 * NG])
        yth = sb("yth", [P, KC, CH])
        ysl = sb("ysl", [P, KC, CH])
        hp = ctx.enter_context(nc.psum_tensor("hp", [P, RING, CH], F32))
        acc = ctx.enter_context(nc.psum_tensor("acc", [P, KC, CH], F32))
        misc = ctx.enter_context(nc.psum_tensor("misc", [P, 2, CH], F32))

        x_landed = [sem(f"x_landed{c}") for c in range(NCH)]
        const_landed = sem("const_landed")
        w_landed = [sem(f"w_landed{s}") for s in range(RING)]
        gate_landed = [sem(f"gate_landed{s}") for s in range(RING)]
        gate_stored = sem("gate_stored")
        out_stored = sem("out_stored")
        dve_link = sem("dve_link")
        power_ready = sem("power_ready")
        var_ready = sem("var_ready")
        rstd_ready = sem("rstd_ready")
        xn_ready = sem("xn_ready")
        xt_ready = sem("xt_ready")
        xf_ready = sem("xf_ready")
        xlo_ready = sem("xlo_ready")
        logits_ready = sem("logits_ready")
        z_ready = sem("z_ready")
        th_ready = sem("th_ready")
        gate_ready = sem("gate_ready")
        gt_ready = sem("gt_ready")
        gts_ready = sem("gts_ready")
        wqhi_ready = sem("wqhi_ready")
        wqlo_ready = sem("wqlo_ready")
        q_ready = sem("q_ready")
        hpre_ready = sem("hpre_ready")
        hh_ready = sem("hh_ready")
        hd_ready = sem("hd_ready")
        hsq_ready = sem("hsq_ready")
        gvar_ready = sem("gvar_ready")
        grstd_ready = sem("grstd_ready")
        hnorm_ready = sem("hnorm_ready")
        hgain_ready = sem("hgain_ready")
        hn_ready = sem("hn_ready")
        whi_ready = sem("whi_ready")
        wlo_ready = sem("wlo_ready")
        l1_done = sem("l1_done")
        relu_done = sem("relu_done")
        gated = sem("gated")
        h_done = sem("h_done")
        hi_done = sem("hi_done")
        lo_done = sem("lo_done")
        acc_done = sem("acc_done")
        yth_ready = sem("yth_ready")
        ysl_ready = sem("ysl_ready")
        ymix_ready = sem("ymix_ready")
        yt_ready = sem("yt_ready")
        rows_ready = sem("rows_ready")

        consts = 16 * 9
        PAIRS = NT // 2
        PC = PAIRS // NCH
        NW = N // GROUP
        WG = GROUP * WCOLS
        hn_tiles = hn[:, :, :, :, :].rearrange("p b j k d -> p (b j k) d")
        block = ctx.enter_context(nc.Block())

        def slot(k):
            return k % RING

        @block.sync
        def _(sp):
            for c in range(NCH):
                sp.dma_start(xs[:, c], x[c].rearrange("j p d -> p j d")).then_inc(x_landed[c], 16)
                if c == 0:
                    for dst, src in ((id_sb[:, :], ident), (wr_sb[:, :, :], wr),
                                     (br_sb[:, :], br.partition_broadcast(P)), (wq_sb[:, :, :], wq),
                                     (hb_sb[:, :], hh_b.partition_broadcast(P)),
                                     (gw_sb[:, :], gn_w.partition_broadcast(P)),
                                     (gb_sb[:, :], gn_b.partition_broadcast(P)),
                                     (cos_sb[:, :, :], cos), (sin_sb[:, :, :], sin)):
                        sp.dma_start(dst, src).then_inc(const_landed, 16)

            def load_w(g, s):
                sp.dma_start(wst[:, s, :], wts[:, bass.ds(g * WG, WG)]).then_inc(w_landed[s], 16)

            for g in range(RING):
                load_w(g, g)
            for c in range(NCH):
                sp.wait_ge(gts_ready, c + 1)
                sp.dma_start(gates[c], gate_t[:, :]).then_inc(gate_stored, 16)
            with sp.Fori(0, (NW - 1) // RING - 1) as i:
                for u in range(RING):
                    sp.wait_ge(wlo_ready, i * RING + (u + 1))
                    load_w(i * RING + (RING + u), u)
            sp.wait_ge(wlo_ready, NW - RING)
            load_w(NW - 1, slot(NW - 1))

            sp.wait_ge(gate_stored, 16 * NCH)

            def load_gate(c, e, s):
                src = gates[c].rearrange("(e j) p -> e (j p)", j=J)
                sp.dma_start(gate_bc[:, s, :], src[bass.ds(e, 1), :].broadcast_to([P, CH]))\
                  .then_inc(gate_landed[s], 16)

            for c in range(NCH):
                if c == 0:
                    for u in range(RING):
                        load_gate(0, u, u)
                with sp.Fori(1 if c == 0 else 0, E // RING) as i:
                    for u in range(RING):
                        sp.wait_ge(gated, i * RING + (c * E + u - RING + 1))
                        load_gate(c, i * RING + u, u)

        @block.gpsimd
        def _(pool):
            nc.gpsimd.memset(power[:, :], -0.5).then_inc(power_ready, 1)
            pool.wait_ge(power_ready, 1)

            def prelude(c):
                pool.wait_ge(var_ready, c + 1)
                nc.gpsimd.tensor_tensor(rstd[:, :], vare[:, :], power[:, 0:J], ALU.pow).then_inc(rstd_ready, 1)

            def recurrent(m):
                pool.wait_ge(gvar_ready, m + 1)
                nc.gpsimd.tensor_tensor(grstd[:, :], gvare[:, :], power[:, :], ALU.pow).then_inc(grstd_ready, 1)
                pool.wait_ge(hnorm_ready, m + 1)
                nc.gpsimd.tensor_tensor(hgain[:, :, :], hnorm[:, :, :],
                                        gw_sb[:, :].unsqueeze(1).broadcast_to([P, 2, D]), ALU.mult)\
                  .then_inc(hgain_ready, 1)
                pool.wait_ge(hgain_ready, m + 1)
                nc.gpsimd.tensor_tensor(hn_tiles[:, 2 * m:2 * m + 2, :], hgain[:, :, :],
                                        gb_sb[:, :].unsqueeze(1).broadcast_to([P, 2, D]), ALU.add)\
                  .then_inc(hn_ready, 1)

            def apply_gate(c, i, u):
                s = slot(c * N + NS + u)
                pool.wait_ge(relu_done, i * RING + (c * N + NS + u + 1))
                pool.wait_ge(gate_landed[u], i * 16 + 16 * (c * E // RING + 1))
                nc.gpsimd.tensor_tensor(relu[:, s, :], relu[:, s, :], gate_bc[:, u, :], ALU.mult)\
                  .then_inc(gated, 1)

            for c in range(NCH):
                prelude(c)
            pool.wait_ge(const_landed, consts)
            for m in range(PAIRS):
                recurrent(m)
            for c in range(NCH):
                with pool.Fori(0, E // RING) as i:
                    for u in range(RING):
                        apply_gate(c, i, u)

        @block.scalar
        def _(act):
            def prelude(c):
                cols = slice(c * CH, (c + 1) * CH)
                for kc in range(KC):
                    act.wait_ge(xt_ready, KC * c + kc + 1)
                    nc.scalar.activation(xhi[:, kc, cols], misc[:, kc, :], ACT.Copy)
                    if c > 0 and kc == 0:
                        act.wait_ge(logits_ready, c)
                    nc.scalar.activation(xf[:, kc, :], misc[:, kc, :], ACT.Copy).then_inc(xf_ready, 1)
                act.wait_ge(z_ready, c + 1)
                nc.scalar.activation(th[:, :, :], zs[:, :, :], ACT.Tanh, scale=0.5).then_inc(th_ready, 1)

            def recurrent(m):
                act.wait_ge(hpre_ready, m + 1)
                nc.scalar.activation(hh[:, :, :], hpre[:, :, :], ACT.Tanh, scale=1.0 / WQ_SCALE)\
                  .then_inc(hh_ready, 1)
                act.wait_ge(hd_ready, m + 1)
                nc.scalar.activation(hsq[:, :, :], hd[:, :, :], ACT.Square).then_inc(hsq_ready, 1)

            def split_w(s, landed, col):
                act.wait_ge(w_landed[s], landed)
                nc.scalar.activation(whi[:, bass.ds(col, WG)], wst[:, s, :], ACT.Copy, scale=W_SCALE)\
                  .then_inc(whi_ready, 1)

            def half(c, i, u):
                k = c * N + u
                act.wait_ge(h_done, i * RING + k)
                nc.scalar.activation(hhi[:, slot(k - 1), :], hp[:, slot(k - 1), :], ACT.Copy).then_inc(hi_done, 1)

            def step(c, i, u):
                k = c * N + u
                act.wait_ge(l1_done, i * RING + (k + 1))
                nc.scalar.activation(relu[:, slot(k), :], hp[:, slot(k), :], ACT.Relu,
                                     scale=1.0 / W_SCALE ** 2 if u < NS else 1.0).then_inc(relu_done, 1)
                if k > 0:
                    half(c, i, u)

            def finish(c):
                act.wait_ge(acc_done, c + 1)
                for kc in range(KC):
                    nc.scalar.activation(yth[:, kc, :], acc[:, kc, :], ACT.Tanh, scale=0.5 / W_SCALE)\
                      .then_inc(yth_ready, 1)

            def store(c):
                act.wait_ge(rows_ready, 2 * (c + 1))
                act.dma_start(out[c].rearrange("j p d -> p j d"), xs[:, c]).then_inc(out_stored, 16)

            act.wait_ge(const_landed, consts)
            nc.scalar.activation(wqhi[:, :, :], wq_sb[:, :, :], ACT.Copy, scale=WQ_SCALE).then_inc(wqhi_ready, 1)
            for c in range(NCH):
                prelude(c)
            split_w(0, 16, 0)
            with act.Fori(0, (NW - 1) // RING) as i:
                for u in range(RING):
                    g = u + 1
                    split_w(slot(g), i * 16 + 16 * (g // RING + 1), i * (RING * WG) + g * WG)
            for m in range(PAIRS):
                recurrent(m)
            for c in range(NCH):
                for u in range(NS + RING):
                    step(c, 0, u)
                    if u == NS - 1 and c > 1:
                        store(c - 2)
                    if u == NS and c > 0:
                        finish(c - 1)
                with act.Fori(1, E // RING) as i:
                    for u in range(NS, NS + RING):
                        step(c, i, u)
            half(NCH, 0, 0)
            finish(NCH - 1)
            for c in (NCH - 2, NCH - 1):
                store(c)
            act.wait_ge(out_stored, 16 * NCH)

        @block.tensor
        def _(pe):
            def prelude_x(c):
                pe.wait_ge(xn_ready, c + 1)
                if c > 0:
                    pe.wait_ge(z_ready, c)
                for kc in range(KC):
                    if c > 0 and kc == 1:
                        pe.wait_ge(gts_ready, c)
                    for j in range(J):
                        mm = nc.tensor.transpose(misc[:, kc, j * P:(j + 1) * P],
                                                 xn[:, j, kc * P:(kc + 1) * P], id_sb[:, :])
                    mm.then_inc(xt_ready, 1)

            def prelude_router(c):
                pe.wait_ge(xf_ready, KC * (c + 1))
                pe.wait_ge(xlo_ready, KC * c + 1)
                for j in range(J):
                    for kc in range(KC):
                        mm = nc.tensor.matmul(misc[:, 0, j * E:(j + 1) * E], xf[:, kc, j * P:(j + 1) * P],
                                              wr_sb[:, kc, :], start=(kc == 0), stop=(kc == KC - 1))
                mm.then_inc(logits_ready, 1)

            def prelude_gate(c):
                pe.wait_ge(gate_ready, c + 1)
                nc.tensor.transpose(misc[:, 1, 0:P], gate[:, :, :].rearrange("p e j -> p (e j)"), id_sb[:, :])\
                  .then_inc(gt_ready, 1)

            def recurrent(m):
                if m >= 2:
                    pe.wait_ge(hpre_ready, m - 1)
                elif m == 0:
                    pe.wait_ge(z_ready, NCH)
                else:
                    pe.wait_ge(gts_ready, NCH)
                for t in range(2):
                    tile = 2 * m + t
                    cols = slice(tile * P, (tile + 1) * P)
                    o = misc[:, m % 2, t * D:(t + 1) * D]
                    for kc in range(KC):
                        nc.tensor.matmul(o, xhi[:, kc, cols], wqhi[:, kc, :], start=(kc == 0), stop=False)
                        nc.tensor.matmul(o, xhi[:, kc, cols], wqlo[:, kc, :], start=False, stop=False)
                        mm = nc.tensor.matmul(o, xlo[:, kc, cols], wqhi[:, kc, :], start=False, stop=(kc == KC - 1))
                mm.then_inc(q_ready, 1)

            def first(c, i, u):
                k = c * N + u
                if k >= RING:
                    pe.wait_ge(lo_done, i * RING + (k - RING + 1))
                cols = slice(c * CH, (c + 1) * CH)
                o = hp[:, slot(k), :]
                for kc in range(KC):
                    at = i * (RING * WCOLS) + (u * WCOLS + kc * M)
                    nc.tensor.matmul(o, whi[:, bass.ds(at, M)], xhi[:, kc, cols], start=(kc == 0), stop=False)
                    nc.tensor.matmul(o, whi[:, bass.ds(at, M)], xlo[:, kc, cols], start=False, stop=False)
                    mm = nc.tensor.matmul(o, wlo[:, bass.ds(at, M)], xhi[:, kc, cols], start=False,
                                          stop=(kc == KC - 1))
                mm.then_inc(l1_done, 1)

            def second(c, i, u):
                peeled = isinstance(i, int)
                if peeled and u < 0:
                    c, u = c - 1, u + N
                k = c * N + u
                pe.wait_ge(lo_done, i * RING + (k + 1))
                begin, end = peeled and u == 0, peeled and u == N - 1
                if begin and c > 0:
                    pe.wait_ge(ysl_ready, KC * c)
                for kc in range(KC):
                    at = i * (RING * WCOLS) + (u * WCOLS + D + kc * P)
                    nc.tensor.matmul(acc[:, kc, :], whi[:, bass.ds(at, P)], hhi[:, slot(k), :],
                                     start=begin, stop=False, skip_group_check=True)
                    nc.tensor.matmul(acc[:, kc, :], wlo[:, bass.ds(at, P)], hhi[:, slot(k), :],
                                     start=False, stop=False, skip_group_check=True)
                for kc in range(KC):
                    at = i * (RING * WCOLS) + (u * WCOLS + D + kc * P)
                    mm = nc.tensor.matmul(acc[:, kc, :], whi[:, bass.ds(at, P)], hlo[:, slot(k), :],
                                          start=False, stop=end, skip_group_check=True)
                if end:
                    mm.then_inc(acc_done, 1)

            def finish(c):
                pe.wait_ge(ymix_ready, KC * (c + 1))
                if c > 0:
                    pe.wait_ge(rows_ready, 2 * c)
                else:
                    pe.wait_ge(hpre_ready, PAIRS)
                for j in range(J):
                    for kc in range(KC):
                        at = (j % 2) * D + kc * P
                        mm = nc.tensor.transpose(misc[:, j // 2, at:at + P],
                                                 ysl[:, kc, j * P:(j + 1) * P], id_sb[:, :])
                mm.then_inc(yt_ready, 1)

            pe.wait_ge(const_landed, consts)
            for c in range(NCH):
                prelude_x(c)
                prelude_router(c)
                prelude_gate(c)
            pe.wait_ge(wqlo_ready, 1)
            pe.wait_ge(xlo_ready, KC * NCH)
            for m in range(PAIRS):
                recurrent(m)
            pe.wait_ge(wlo_ready, NW)
            for c in range(NCH):
                for u in range(NS + RING):
                    first(c, 0, u)
                    if c * N + u >= LAG:
                        second(c, 0, u - LAG)
                if c > 0:
                    finish(c - 1)
                with pe.Fori(1, E // RING) as i:
                    for u in range(NS, NS + RING):
                        first(c, i, u)
                        second(c, i, u - LAG)
            for u in range(N - LAG, N):
                second(NCH - 1, 0, u)
            finish(NCH - 1)

        @block.vector
        def _(dve):
            links = [0]

            def link(ins):
                links[0] += 1
                ins.then_inc(dve_link, 1)
                dve.wait_ge(dve_link, links[0])

            def prelude_x(c):
                dve.wait_ge(x_landed[c], 16)
                for j in range(J):
                    last = nc.vector.bn_stats(stats[:, j, :], xs[:, c, j, :])
                link(last)
                for j in range(J):
                    last = nc.vector.bn_aggr(mv[:, j, :], stats[:, j, :])
                link(last)
                nc.vector.tensor_scalar(vare[:, :], mv[:, :, 1], 1e-5, None, ALU.add).then_inc(var_ready, 1)
                dve.wait_ge(rstd_ready, c + 1)
                if c > 0:
                    dve.wait_ge(xt_ready, KC * c)
                for j in range(J):
                    last = nc.vector.tensor_scalar(xn[:, j, :], xs[:, c, j, :], mv[:, j, 0:1], rstd[:, j:j + 1],
                                                   ALU.subtract, ALU.mult)
                last.then_inc(xn_ready, 1)
                for kc in range(KC):
                    dve.wait_ge(xf_ready, KC * c + kc + 1)
                    cols = slice(c * CH, (c + 1) * CH)
                    nc.vector.tensor_tensor(xlo[:, kc, cols], misc[:, kc, :], xhi[:, kc, cols], ALU.subtract)\
                      .then_inc(xlo_ready, 1)

            def prelude_route(c):
                dve.wait_ge(logits_ready, c + 1)
                nc.vector.tensor_tensor(zs[:, :, :], misc[:, 0, 0:J * E].rearrange("p (j e) -> p j e", j=J),
                                        br_sb[:, :].unsqueeze(1).broadcast_to([P, J, E]), ALU.add)\
                  .then_inc(z_ready, 1)
                dve.wait_ge(th_ready, c + 1)
                link(nc.vector.tensor_scalar(ss[:, :, :], th[:, :, :], 0.5, 0.5, ALU.mult, ALU.add))
                s4 = ss[:, :, :].rearrange("p j (g e) -> p (j g) e", e=EG)
                nc.vector.tensor_tensor(pairs[:, :, 0:3], s4[:, :, 0:3], s4[:, :, 1:4], ALU.add)
                nc.vector.tensor_tensor(pairs[:, :, 3:5], s4[:, :, 0:2], s4[:, :, 2:4], ALU.add)
                link(nc.vector.tensor_tensor(pairs[:, :, 5:6], s4[:, :, 0:1], s4[:, :, 3:4], ALU.add))
                link(nc.vector.tensor_reduce(gsum[:, :, 0:G],
                                             pairs[:, :, :].rearrange("p (j g) s -> p j g s", j=J), AX.X, ALU.max))
                for j in range(J):
                    last = nc.vector.max(top_g[:, j, :], gsum[:, j, 0:G])
                link(last)
                link(nc.vector.memset(top_g[:, :, KG:8], NONE))
                for j in range(J):
                    last = nc.vector.match_replace(gmark[:, j, :], top_g[:, j, :], gsum[:, j, :], MARK)
                link(last)
                link(nc.vector.tensor_scalar(gmask[:, :, :], gmark[:, :, 0:G], MARK, None, ALU.is_ge))
                gm = gmask[:, :, :].unsqueeze(3).broadcast_to([P, J, G, EG])
                link(nc.vector.tensor_tensor(masked[:, :, 0:E].rearrange("p j (g e) -> p j g e", e=EG),
                                             ss[:, :, :].rearrange("p j (g e) -> p j g e", e=EG), gm, ALU.mult))
                for j in range(J):
                    last = nc.vector.max(top_e[:, j, :], masked[:, j, 0:E])
                link(last)
                link(nc.vector.memset(top_e[:, :, K:8], NONE))
                for j in range(J):
                    last = nc.vector.match_replace(emark[:, j, :], top_e[:, j, :], masked[:, j, :], MARK)
                link(last)
                link(nc.vector.scalar_tensor_tensor(sel[:, :, :], emark[:, :, 0:E], MARK, ss[:, :, :],
                                                    ALU.is_ge, ALU.mult))
                link(nc.vector.tensor_reduce(wsum[:, :], sel[:, :, :], AX.X, ALU.add))
                link(nc.vector.tensor_scalar(wsum[:, :], wsum[:, :], 1e-20, None, ALU.add))
                link(nc.vector.reciprocal(wrec[:, :], wsum[:, :]))
                nc.vector.scalar_tensor_tensor(gate[:, :, :].rearrange("p e j -> p j e"), sel[:, :, :],
                                               SCALE / W_SCALE ** 2,
                                               wrec[:, :].unsqueeze(2).broadcast_to([P, J, E]),
                                               ALU.mult, ALU.mult).then_inc(gate_ready, 1)
                dve.wait_ge(gt_ready, c + 1)
                if c > 0:
                    dve.wait_ge(gate_stored, 16 * c)
                nc.vector.tensor_copy(gate_t[:, :], misc[:, 1, 0:P]).then_inc(gts_ready, 1)

            def recurrent(m):
                q = misc[:, m % 2, :].rearrange("p (t c) -> p t c", t=2)
                t0 = 2 * m % (T // P)
                dve.wait_ge(q_ready, m + 1)
                cs, sn = cos_sb[:, t0:t0 + 2, :], sin_sb[:, t0:t0 + 2, :]
                nc.vector.tensor_tensor(ra[:, :, :], q[:, :, 0:ROPE], cs, ALU.mult)
                nc.vector.tensor_tensor(rb[:, :, 0:ROPE:2], q[:, :, 1:ROPE:2], sn[:, :, 0:ROPE:2], ALU.mult)
                link(nc.vector.tensor_tensor(rb[:, :, 1:ROPE:2], q[:, :, 0:ROPE:2], sn[:, :, 1:ROPE:2], ALU.mult))
                link(nc.vector.tensor_tensor(ra[:, :, :], ra[:, :, :], rb[:, :, :], ALU.add))
                if m > 0:
                    dve.wait_ge(hh_ready, m)
                hb = hbs[:, :].unsqueeze(1).broadcast_to([P, 2, D])
                nc.vector.scalar_tensor_tensor(hpre[:, :, 0:ROPE], ra[:, :, :], 0.0, hb[:, :, 0:ROPE],
                                               ALU.max, ALU.add)
                nc.vector.scalar_tensor_tensor(hpre[:, :, ROPE:D], q[:, :, ROPE:D], 0.0, hb[:, :, ROPE:D],
                                               ALU.max, ALU.add).then_inc(hpre_ready, 1)
                dve.wait_ge(hh_ready, m + 1)
                grouped = lambda a: a[:, :, :].rearrange("p t (g w) -> p (t g) w", w=GW)
                link(nc.vector.tensor_reduce(gmean[:, :], grouped(hh), AX.X, ALU.add))
                link(nc.vector.tensor_scalar(gmean[:, :], gmean[:, :], -1.0 / GW, None, ALU.mult))
                nc.vector.tensor_tensor(grouped(hd), grouped(hh),
                                        gmean[:, :].unsqueeze(2).broadcast_to([P, 2 * NG, GW]), ALU.add)\
                  .then_inc(hd_ready, 1)
                dve.wait_ge(hsq_ready, m + 1)
                link(nc.vector.tensor_reduce(gvar[:, :], grouped(hsq), AX.X, ALU.add))
                nc.vector.tensor_scalar(gvare[:, :], gvar[:, :], 1.0 / GW, 1e-5, ALU.mult, ALU.add)\
                  .then_inc(gvar_ready, 1)
                dve.wait_ge(grstd_ready, m + 1)
                if m > 0:
                    dve.wait_ge(hgain_ready, m)
                nc.vector.tensor_tensor(grouped(hnorm), grouped(hd),
                                        grstd[:, :].unsqueeze(2).broadcast_to([P, 2 * NG, GW]), ALU.mult)\
                  .then_inc(hnorm_ready, 1)

            def split_w(s, i, g):
                dve.wait_ge(whi_ready, i * RING + (g + 1))
                cols = bass.ds(i * (RING * WG) + g * WG, WG)
                nc.vector.scalar_tensor_tensor(wlo[:, cols], wst[:, s, :], W_SCALE, whi[:, cols],
                                               ALU.mult, ALU.subtract).then_inc(wlo_ready, 1)

            def half(c, i, u):
                k = c * N + u
                s = slot(k - 1)
                dve.wait_ge(hi_done, i * RING + k)
                nc.vector.tensor_tensor(hlo[:, s, :], hp[:, s, :], hhi[:, s, :], ALU.subtract)\
                  .then_inc(lo_done, 1)

            def step(c, i, u):
                k = c * N + u
                if k > 0:
                    half(c, i, u)
                if u < NS:
                    dve.wait_ge(relu_done, k + 1)
                else:
                    dve.wait_ge(gated, i * RING + (c * E + u - NS + 1))
                s = slot(k)
                nc.vector.tensor_tensor(hp[:, s, :], relu[:, s, :], hp[:, s, :], ALU.mult).then_inc(h_done, 1)

            def finish_sum(c):
                b, half_ch = c // (NCH // B), c % (NCH // B)
                for kc in range(KC):
                    dve.wait_ge(yth_ready, KC * c + kc + 1)
                    nc.vector.scalar_tensor_tensor(ysl[:, kc, :], yth[:, kc, :], 1.0, acc[:, kc, :],
                                                   ALU.add, ALU.mult).then_inc(ysl_ready, 1)
                dve.wait_ge(ysl_ready, KC * (c + 1))
                dve.wait_ge(hn_ready, PAIRS // B * (b + 1))
                for kc in range(KC):
                    branch = hn[:, b, :, kc, half_ch * P:(half_ch + 1) * P].rearrange("p j q -> p q j")
                    nc.vector.scalar_tensor_tensor(ysl[:, kc, :].rearrange("p (q j) -> p q j", j=J),
                                                   ysl[:, kc, :].rearrange("p (q j) -> p q j", j=J),
                                                   0.5 / W_SCALE, branch, ALU.mult, ALU.mult)\
                      .then_inc(ymix_ready, 1)

            def finish_rows(c):
                dve.wait_ge(yt_ready, c + 1)
                for h in range(2):
                    nc.vector.tensor_tensor(xs[:, c, 2 * h:2 * h + 2, :],
                                            misc[:, h, :].rearrange("p (j d) -> p j d", j=2),
                                            xs[:, c, 2 * h:2 * h + 2, :], ALU.add).then_inc(rows_ready, 1)

            nc.vector.memset(gsum[:, :, G:2 * G], NONE)
            link(nc.vector.memset(masked[:, :, E:E + 8], NONE))
            for c in range(NCH):
                prelude_x(c)
                if c == 0:
                    dve.wait_ge(const_landed, consts)
                    nc.vector.tensor_scalar(hbs[:, :], hb_sb[:, :], WQ_SCALE, None, ALU.mult)
                    dve.wait_ge(wqhi_ready, 1)
                    nc.vector.scalar_tensor_tensor(wqlo[:, :, :], wq_sb[:, :, :], WQ_SCALE, wqhi[:, :, :],
                                                   ALU.mult, ALU.subtract).then_inc(wqlo_ready, 1)
                prelude_route(c)
            split_w(0, 0, 0)
            with dve.Fori(0, (NW - 1) // RING) as i:
                for u in range(RING):
                    split_w(slot(u + 1), i, u + 1)
            for m in range(PAIRS):
                recurrent(m)
            for c in range(NCH):
                for u in range(NS + RING):
                    step(c, 0, u)
                    if u == NS and c > 0:
                        finish_sum(c - 1)
                with dve.Fori(1, E // RING) as i:
                    for u in range(NS, NS + RING):
                        step(c, i, u)
                if c > 0:
                    finish_rows(c - 1)
            half(NCH, 0, 0)
            finish_sum(NCH - 1)
            finish_rows(NCH - 1)


def kernel(L0_attn_X, L0_attn_S_n, L0_attn_W_Q, L0_attn_hh_b, L0_attn_gn_weight, L0_attn_gn_bias,
           L0_ffn_Wr, L0_ffn_br, L0_ffn_W1, L0_ffn_W2, L0_ffn_Ws1, L0_ffn_Ws2):
    import concourse.bacc as bacc
    from concourse.bass_utils import run_bass_kernel_spmd

    arr = lambda a: np.asarray(a)
    flat = np.ascontiguousarray
    w1 = np.concatenate([arr(L0_ffn_Ws1).reshape(NS, M, D), arr(L0_ffn_W1)])
    w2 = np.concatenate([arr(L0_ffn_Ws2).reshape(D, NS, M).transpose(1, 0, 2), arr(L0_ffn_W2)])
    w1 = w1.reshape(N, M, KC, P).transpose(3, 0, 2, 1).reshape(P, N, D)
    w2 = w2.transpose(2, 0, 1)
    inv_freq = np.float32(1.0) / np.power(np.float32(10000.0), np.arange(0, ROPE, 2, dtype=np.float32) / np.float32(ROPE))
    angle = np.repeat(np.arange(T, dtype=np.float32)[:, None] * inv_freq.astype(np.float32)[None, :], 2, axis=1)
    by_tile = lambda a: flat(a.astype(np.float32).reshape(T // P, P, ROPE).transpose(1, 0, 2))
    sign = np.tile(np.array([-1.0, 1.0]), ROPE // 2)
    arrays = {
        "x": flat(arr(L0_attn_X).reshape(NCH, J, P, D)),
        "wts": flat(np.concatenate([w1, w2], axis=2).reshape(P, N * WCOLS)),
        "wr": flat(arr(L0_ffn_Wr).T.reshape(KC, P, E).transpose(1, 0, 2)),
        "br": arr(L0_ffn_br),
        "wq": flat(arr(L0_attn_W_Q).reshape(KC, P, D).transpose(1, 0, 2)),
        "hh_b": arr(L0_attn_hh_b),
        "gn_w": arr(L0_attn_gn_weight),
        "gn_b": arr(L0_attn_gn_bias),
        "cos": by_tile(np.cos(angle.astype(np.float64))),
        "sin": by_tile(np.sin(angle.astype(np.float64)) * sign),
        "ident": np.eye(P, dtype=np.float32),
    }
    nc = bacc.Bacc("TRN2", target_bir_lowering=False, num_devices=1)
    args = [nc.dram_tensor(f"in_{k}", a.shape, F32, kind="ExternalInput").ap() for k, a in arrays.items()]
    out = nc.dram_tensor("out", (NCH, J, P, D), F32, kind="ExternalOutput").ap()
    gates = nc.dram_tensor("gates", (NCH, P, P), F32, kind="Internal").ap()
    build(nc, *args, out, gates)
    r = run_bass_kernel_spmd(nc, [{f"in_{k}": a for k, a in arrays.items()}], core_ids=[0])
    return r.results[0]["out"].reshape(B, T, D)
```

```python
import numpy as np
import concourse.bass as bass
from concourse import mybir
from contextlib import ExitStack
from functools import partial

ALU = mybir.AluOpType
ACT = mybir.ActivationFunctionType
AX = mybir.AxisListType
F32 = mybir.dt.float32
F16 = mybir.dt.float16
I32 = mybir.dt.int32

P = 128
B, T, D = 2, 1024, 256
KC = D // P
E, M = 32, 128
SH = 256
NS = SH // M
N = NS + E
G, EG = 8, E // 8
KG, K = 4, 6
CH = 512
NCH = B * T // CH
J = CH // P
NT = B * T // P
NG, GW = 32, 8
ROPE = 64
WCOLS = D + D
RING = 4
BODY = 8
LAG = 3
GROUP = 2
AHEAD = 4
MAGIC = 0x5f3759df

W_SCALE = 64.0
WQ_SCALE = 256.0
SCALE = 2.5
MARK = 4.0
NONE = -1.0


def build(nc, x, wts, wr, br, wq, hh_b, gn_w, gn_b, cos, sin, ident, out, gates):
    with ExitStack() as ctx:
        def sb(name, shape, dt=F32):
            return ctx.enter_context(nc.sbuf_tensor(name, shape, dt))

        def sem(name):
            return ctx.enter_context(nc.semaphore(name))

        xs = sb("xs", [P, NT, D])
        xhi = sb("xhi", [P, KC, B * T], F16)
        xlo = sb("xlo", [P, KC, B * T], F16)
        whi = sb("whi", [P, N * WCOLS], F16)
        wlo = sb("wlo", [P, N * WCOLS], F16)
        hn = sb("hn", [P, NT, D])
        wr_sb = sb("wr_sb", [P, KC, E])
        br_sb = sb("br_sb", [P, E])
        wq_sb = sb("wq_sb", [P, KC, D])
        wqhi = sb("wqhi", [P, KC, D], F16)
        wqlo = sb("wqlo", [P, KC, D], F16)
        hb_sb = sb("hb_sb", [P, D])
        hbs = sb("hbs", [P, D])
        gw_sb = sb("gw_sb", [P, D])
        gb_sb = sb("gb_sb", [P, D])
        cos_sb = sb("cos_sb", [P, T // P, ROPE])
        sin_sb = sb("sin_sb", [P, T // P, ROPE])
        id_sb = sb("id_sb", [P, P])
        power = sb("power", [P, J])
        wst = sb("wst", [P, RING, GROUP * WCOLS])
        gate_bc = sb("gate_bc", [P, RING, CH])
        relu = sb("relu", [P, RING, CH])
        hhi = sb("hhi", [P, RING, CH], F16)
        hlo = sb("hlo", [P, RING, CH], F16)
        xn = sb("xn", [P, J, D])
        xf = sb("xf", [P, KC, CH])
        stats = sb("stats", [P, J, 6])
        mv = sb("mv", [P, J, 2])
        vare = sb("vare", [P, J])
        rstd = sb("rstd", [P, J])
        zs = sb("zs", [P, J, E])
        th = sb("th", [P, J, E])
        ss = sb("ss", [P, J, E])
        pairs = sb("pairs", [P, J * G, 6])
        gsum = sb("gsum", [P, J, 2 * G])
        top_g = sb("top_g", [P, J, 8])
        gmark = sb("gmark", [P, J, 2 * G])
        gmask = sb("gmask", [P, J, G])
        masked = sb("masked", [P, J, E + 8])
        top_e = sb("top_e", [P, J, 8])
        emark = sb("emark", [P, J, E + 8])
        sel = sb("sel", [P, J, E])
        wsum = sb("wsum", [P, J])
        wrec = sb("wrec", [P, J])
        gate = sb("gate", [P, J, E])
        gate_t = sb("gate_t", [P, P])
        ra = sb("ra", [P, ROPE])
        rb = sb("rb", [P, ROPE])
        hpre = sb("hpre", [P, D])
        hh = sb("hh", [P, D])
        hd = sb("hd", [P, D])
        hsq = sb("hsq", [P, D])
        hnorm = sb("hnorm", [P, D])
        hgain = sb("hgain", [P, D])
        gmean = sb("gmean", [P, NG])
        gvar = sb("gvar", [P, NG])
        gvare = sb("gvare", [P, NG])
        ghalf = sb("ghalf", [P, NG], I32)
        grstd = sb("grstd", [P, NG])
        gnewt = sb("gnewt", [P, NG])
        yth = sb("yth", [P, KC, CH])
        ysl = sb("ysl", [P, 2, KC, CH])
        hp = ctx.enter_context(nc.psum_tensor("hp", [P, RING, CH], F32))
        acc = ctx.enter_context(nc.psum_tensor("acc", [P, KC, CH], F32))
        bank_a = ctx.enter_context(nc.psum_tensor("bank_a", [P, CH], F32))
        bank_b = ctx.enter_context(nc.psum_tensor("bank_b", [P, CH], F32))

        x_landed = [sem(f"x_landed{c}") for c in range(NCH)]
        const_landed = sem("const_landed")
        w_landed = [sem(f"w_landed{s}") for s in range(RING)]
        gate_landed = [sem(f"gate_landed{s}") for s in range(RING)]
        gate_stored = sem("gate_stored")
        out_stored = sem("out_stored")
        var_ready = sem("var_ready")
        rstd_ready = sem("rstd_ready")
        xn_ready = sem("xn_ready")
        xt_ready = sem("xt_ready")
        xf_ready = sem("xf_ready")
        xlo_ready = sem("xlo_ready")
        logits_ready = sem("logits_ready")
        z_ready = sem("z_ready")
        th_ready = sem("th_ready")
        gate_ready = sem("gate_ready")
        gt_ready = sem("gt_ready")
        gts_ready = sem("gts_ready")
        wqhi_ready = sem("wqhi_ready")
        wqlo_ready = sem("wqlo_ready")
        q_ready = sem("q_ready")
        hpre_ready = sem("hpre_ready")
        hh_ready = sem("hh_ready")
        hd_ready = sem("hd_ready")
        hsq_ready = sem("hsq_ready")
        seed_ready = sem("seed_ready")
        grstd_ready = sem("grstd_ready")
        hnorm_ready = sem("hnorm_ready")
        hgain_ready = sem("hgain_ready")
        hn_ready = sem("hn_ready")
        whi_ready = sem("whi_ready")
        wlo_ready = sem("wlo_ready")
        l1_done = sem("l1_done")
        relu_done = sem("relu_done")
        gated = sem("gated")
        h_done = sem("h_done")
        hi_done = sem("hi_done")
        lo_done = sem("lo_done")
        acc_done = sem("acc_done")
        yth_ready = sem("yth_ready")
        ysl_ready = sem("ysl_ready")
        ymix_ready = sem("ymix_ready")
        yt_ready = sem("yt_ready")
        rows_ready = sem("rows_ready")

        consts = 16 * 9
        NW = N // GROUP
        WG = GROUP * WCOLS
        ITERS = E // BODY
        BATCHES = NT - J + 1
        assert ITERS == J and BODY % RING == 0
        block = ctx.enter_context(nc.Block())

        def slot(k):
            return k % RING

        def looped(c):
            return 1, ITERS - 1 if c in (0, NCH - 2) else ITERS

        def routes(c):
            return c < NCH - 1

        def normalises(c, i):
            return c < NCH - 2 or (c == NCH - 2 and not (isinstance(i, int) and i == ITERS - 1))

        def iterate(engine, c, body):
            first, last = looped(c)
            body(c, 0)
            with engine.Fori(first, last) as i:
                body(c, i)
            for i in range(last, ITERS):
                body(c, i)

        def settle(engine, _):
            engine.drain()

        @block.sync
        def _(sp):
            def load_x(c):
                sp.dma_start(xs[:, c * J:(c + 1) * J, :], x[c].rearrange("j p d -> p j d"))\
                  .then_inc(x_landed[c], 16)

            def load_w(g, s):
                sp.dma_start(wst[:, s, :], wts[:, bass.ds(g * WG, WG)]).then_inc(w_landed[s], 16)

            load_x(0)
            for dst, src in ((id_sb[:, :], ident), (wr_sb[:, :, :], wr), (br_sb[:, :], br.partition_broadcast(P)),
                             (wq_sb[:, :, :], wq), (hb_sb[:, :], hh_b.partition_broadcast(P)),
                             (gw_sb[:, :], gn_w.partition_broadcast(P)), (gb_sb[:, :], gn_b.partition_broadcast(P)),
                             (cos_sb[:, :, :], cos), (sin_sb[:, :, :], sin)):
                sp.dma_start(dst, src).then_inc(const_landed, 16)
            for g in range(RING):
                load_w(g, g)
            for c in range(1, NCH):
                load_x(c)

            def load_gate(c, e, s):
                sp.dma_start(gate_bc[:, s, :], gates[c, bass.ds(e, 1), :].broadcast_to([P, CH]))\
                  .then_inc(gate_landed[s], 16)

            def iteration(c, i):
                for s in range(BODY):
                    if not (isinstance(i, int) and c == 0 and i == 0 and s < RING):
                        sp.wait_ge(gated, i * BODY + (c * E + s - RING + 1))
                    load_gate(c, i * BODY + s, slot(s))
                    if s % 2 and c == 0 and not (isinstance(i, int) and i == ITERS - 1 and s > 1):
                        q = s // 2
                        sp.wait_ge(wlo_ready, i * (BODY // GROUP) + (q + 1))
                        load_w(i * (BODY // GROUP) + (RING + q), q)

            for c in range(NCH):
                sp.wait_ge(gate_stored, 16 * J * (c + 1))
                iterate(sp, c, iteration)

        @block.gpsimd
        def _(pool):
            settled = partial(settle, pool)

            settled(nc.gpsimd.memset(power[:, :], -0.5))

            def row_rstd(n, nj):
                pool.wait_ge(var_ready, n + 1)
                nc.gpsimd.tensor_tensor(rstd[:, 0:nj], vare[:, 0:nj], power[:, 0:nj], ALU.pow)\
                  .then_inc(rstd_ready, 1)

            def group_rstd(t):
                pool.wait_ge(seed_ready, t + 1)
                for n in range(3):
                    settled(nc.gpsimd.tensor_tensor(gnewt[:, :], grstd[:, :], grstd[:, :], ALU.mult))
                    settled(nc.gpsimd.tensor_tensor(gnewt[:, :], gnewt[:, :], gvare[:, :], ALU.mult))
                    settled(nc.gpsimd.tensor_scalar(gnewt[:, :], gnewt[:, :], -0.5, 1.5, ALU.mult, ALU.add))
                    last = nc.gpsimd.tensor_tensor(grstd[:, :], grstd[:, :], gnewt[:, :], ALU.mult)
                    if n < 2:
                        settled(last)
                last.then_inc(grstd_ready, 1)

            def group_affine(t):
                pool.wait_ge(hnorm_ready, t + 1)
                nc.gpsimd.tensor_tensor(hgain[:, :], hnorm[:, :], gw_sb[:, :], ALU.mult).then_inc(hgain_ready, 1)
                pool.wait_ge(hgain_ready, t + 1)
                nc.gpsimd.tensor_tensor(hn[:, bass.ds(t, 1), :].squeeze(1), hgain[:, :], gb_sb[:, :], ALU.add)\
                  .then_inc(hn_ready, 1)

            def iteration(c, i):
                t = i + c * J
                for s in range(BODY):
                    k = c * N + NS + s
                    pool.wait_ge(relu_done, i * BODY + (k + 1))
                    pool.wait_ge(gate_landed[slot(s)], i * (16 * BODY // RING) + 16 * ((c * E + s) // RING + 1))
                    nc.gpsimd.tensor_tensor(relu[:, slot(k), :], relu[:, slot(k), :], gate_bc[:, slot(s), :],
                                            ALU.mult).then_inc(gated, 1)
                    if s == 1 and normalises(c, i):
                        row_rstd(i + (c * J + 2), 1)
                    if s == 6:
                        group_rstd(t)
                    if s == 7:
                        group_affine(t)

            row_rstd(0, J)
            row_rstd(1, 1)
            pool.wait_ge(const_landed, consts)
            for c in range(NCH):
                iterate(pool, c, iteration)

        @block.scalar
        def _(act):
            def copy_x(n, t, nj):
                cols = bass.ds(t * P, nj * P)
                act.wait_ge(xt_ready, n + 1)
                for kc, (dst, half) in enumerate(((bank_a, 0), (bank_b, 0)) if nj > 1 else ((bank_b, 0), (bank_b, 1))):
                    src = dst[:, half * P:half * P + nj * P]
                    nc.scalar.activation(xhi[:, kc, cols], src, ACT.Copy)
                    last = nc.scalar.activation(xf[:, kc, 0:nj * P], src, ACT.Copy)
                last.then_inc(xf_ready, 1)

            def tanh_z(n, nj):
                act.wait_ge(z_ready, n + 1)
                nc.scalar.activation(th[:, 0:nj, :], zs[:, 0:nj, :], ACT.Tanh, scale=0.5).then_inc(th_ready, 1)

            def store_gates(n, c, j, nj):
                act.wait_ge(gt_ready, n + 1)
                if nj == 1:
                    act.wait_ge(gate_stored, (n + (J - 1)) * 16)
                nc.scalar.activation(gate_t[0:nj * E, :], bank_a[0:nj * E, 0:P], ACT.Copy).then_inc(gts_ready, 1)
                act.wait_ge(gts_ready, n + 1)
                for q in range(nj):
                    act.dma_start(gates[c, :, bass.ds((j + q) * P, P)], gate_t[q * E:(q + 1) * E, :])\
                       .then_inc(gate_stored, 16)

            def split_w(g, s, landed):
                act.wait_ge(w_landed[s], landed)
                nc.scalar.activation(whi[:, bass.ds(g * WG, WG)], wst[:, s, :], ACT.Copy, scale=W_SCALE)\
                  .then_inc(whi_ready, 1)

            def half(k, s):
                act.wait_ge(h_done, k)
                nc.scalar.activation(hhi[:, s, :], hp[:, s, :], ACT.Copy).then_inc(hi_done, 1)

            def step(c, i, u):
                k = c * N + u
                act.wait_ge(l1_done, i * BODY + (k + 1))
                nc.scalar.activation(relu[:, slot(k), :], hp[:, slot(k), :], ACT.Relu,
                                     scale=1.0 / W_SCALE ** 2 if u < NS else 1.0).then_inc(relu_done, 1)
                if k > 0:
                    half(i * BODY + k, slot(k - 1))

            def finish(c):
                act.wait_ge(acc_done, c + 1)
                for kc in range(KC):
                    nc.scalar.activation(yth[:, kc, :], acc[:, kc, :], ACT.Tanh, scale=0.5 / W_SCALE)\
                      .then_inc(yth_ready, 1)

            def store(c):
                act.wait_ge(rows_ready, 2 * (c + 1))
                act.dma_start(out[c].rearrange("j p d -> p j d"), xs[:, c * J:(c + 1) * J, :])\
                   .then_inc(out_stored, 16)

            def iteration(c, i):
                t = i + c * J
                for s in range(BODY):
                    step(c, i, NS + s)
                    if s == 0 and isinstance(i, int) and i == 0 and c > 0:
                        finish(c - 1)
                    if s == 2:
                        if routes(c):
                            tanh_z(i + (c * J + 1), 1)
                        act.wait_ge(hpre_ready, t + 1)
                        nc.scalar.activation(hh[:, :], hpre[:, :], ACT.Tanh, scale=1.0 / WQ_SCALE)\
                          .then_inc(hh_ready, 1)
                    if s == 4:
                        act.wait_ge(hd_ready, t + 1)
                        nc.scalar.activation(hsq[:, :], hd[:, :], ACT.Square).then_inc(hsq_ready, 1)
                    if s == 6 and normalises(c, i):
                        copy_x(i + (c * J + 2), i + ((c + 1) * J + 1), 1)
                    if s == 7 and routes(c):
                        store_gates(i + (c * J + 1), c + 1, i, 1)
                    if s == 7 and isinstance(i, int) and i == 0 and c > 1:
                        store(c - 2)
                    if s % 2 and c == 0 and not (isinstance(i, int) and i == ITERS - 1 and s > 1):
                        g = AHEAD + s // 2
                        split_w(i * (BODY // GROUP) + g, slot(g), i * 16 + 16 * (g // RING + 1))

            act.wait_ge(xt_ready, 1)
            copy_x(0, 0, J)
            nc.scalar.activation(wqhi[:, :, :], wq_sb[:, :, :], ACT.Copy, scale=WQ_SCALE).then_inc(wqhi_ready, 1)
            split_w(0, 0, 16)
            tanh_z(0, J)
            store_gates(0, 0, 0, J)
            split_w(1, 1, 16)
            copy_x(1, J, 1)
            for c in range(NCH):
                for u in range(NS):
                    step(c, 0, u)
                    if c == 0:
                        split_w(GROUP + u, GROUP + u, 16)
                iterate(act, c, iteration)
            half(NCH * N, slot(NCH * N - 1))
            finish(NCH - 1)
            for c in (NCH - 2, NCH - 1):
                store(c)
            act.wait_ge(out_stored, 16 * NCH)

        @block.tensor
        def _(pe):
            def transpose_x(n, nj):
                pe.wait_ge(xn_ready, n + 1)
                if nj == 1:
                    pe.wait_ge(z_ready, n)
                for kc, (dst, half) in enumerate(((bank_a, 0), (bank_b, 0)) if nj > 1 else ((bank_b, 0), (bank_b, 1))):
                    for j in range(nj):
                        at = (half + j) * P
                        mm = nc.tensor.transpose(dst[:, at:at + P], xn[:, j, kc * P:(kc + 1) * P], id_sb[:, :])
                mm.then_inc(xt_ready, 1)

            def router(n, nj):
                pe.wait_ge(xlo_ready, n + 1)
                for j in range(nj):
                    for kc in range(KC):
                        mm = nc.tensor.matmul(bank_b[:, j * E:(j + 1) * E], xf[:, kc, j * P:(j + 1) * P],
                                              wr_sb[:, kc, :], start=(kc == 0), stop=(kc == KC - 1))
                mm.then_inc(logits_ready, 1)

            def transpose_gates(n, nj):
                pe.wait_ge(gate_ready, n + 1)
                nc.tensor.transpose(bank_a[0:nj * E, 0:P], gate[:, 0:nj, :].rearrange("p j e -> p (j e)"),
                                    id_sb[:, :]).then_inc(gt_ready, 1)

            def recurrent(c, i):
                t = i + c * J
                pe.wait_ge(gts_ready, i + (c * J + 1) if routes(c) else BATCHES)
                if not (isinstance(t, int) and t == 0):
                    pe.wait_ge(hpre_ready, t)
                cols = bass.ds(t * P, P)
                for kc in range(KC):
                    nc.tensor.matmul(bank_a[:, 0:D], xhi[:, kc, cols], wqhi[:, kc, :], start=(kc == 0), stop=False)
                    nc.tensor.matmul(bank_a[:, 0:D], xhi[:, kc, cols], wqlo[:, kc, :], start=False, stop=False)
                    mm = nc.tensor.matmul(bank_a[:, 0:D], xlo[:, kc, cols], wqhi[:, kc, :], start=False,
                                          stop=(kc == KC - 1))
                mm.then_inc(q_ready, 1)

            def first(c, i, u):
                k = c * N + u
                if k >= RING:
                    pe.wait_ge(lo_done, i * BODY + (k - RING + 1))
                cols = slice(c * CH, (c + 1) * CH)
                o = hp[:, slot(k), :]
                for kc in range(KC):
                    at = bass.ds(i * (BODY * WCOLS) + (u * WCOLS + kc * M), M)
                    nc.tensor.matmul(o, whi[:, at], xhi[:, kc, cols], start=(kc == 0), stop=False)
                    nc.tensor.matmul(o, whi[:, at], xlo[:, kc, cols], start=False, stop=False)
                    mm = nc.tensor.matmul(o, wlo[:, at], xhi[:, kc, cols], start=False, stop=(kc == KC - 1))
                mm.then_inc(l1_done, 1)

            def second(c, i, u):
                peeled = isinstance(i, int)
                if peeled and i == 0 and u < 0:
                    c, u = c - 1, u + N
                k = c * N + u
                pe.wait_ge(lo_done, i * BODY + (k + 1))
                begin, end = peeled and i == 0 and u == 0, peeled and u == N - 1
                if begin and c > 0:
                    pe.wait_ge(ysl_ready, KC * c)
                for kc in range(KC):
                    at = bass.ds(i * (BODY * WCOLS) + (u * WCOLS + D + kc * P), P)
                    nc.tensor.matmul(acc[:, kc, :], whi[:, at], hhi[:, slot(k), :],
                                     start=begin, stop=False, skip_group_check=True)
                    nc.tensor.matmul(acc[:, kc, :], wlo[:, at], hhi[:, slot(k), :],
                                     start=False, stop=False, skip_group_check=True)
                for kc in range(KC):
                    at = bass.ds(i * (BODY * WCOLS) + (u * WCOLS + D + kc * P), P)
                    mm = nc.tensor.matmul(acc[:, kc, :], whi[:, at], hlo[:, slot(k), :],
                                          start=False, stop=end, skip_group_check=True)
                if end:
                    mm.then_inc(acc_done, 1)

            def transpose_rows(c):
                pe.wait_ge(ymix_ready, KC * (c + 1))
                for h, dst in enumerate((bank_a, bank_b)):
                    for q in range(2 * KC):
                        j, kc = 2 * h + q // KC, q % KC
                        mm = nc.tensor.transpose(dst[:, q * P:(q + 1) * P], ysl[:, c % 2, kc, j * P:(j + 1) * P],
                                                 id_sb[:, :])
                    mm.then_inc(yt_ready, 1)

            def iteration(c, i):
                begins = isinstance(i, int) and i == 0
                n = i + (c * J + 1)
                for s in range(BODY):
                    u = NS + s
                    first(c, i, u)
                    if not (c == 0 and begins and u < LAG):
                        second(c, i, u - LAG)
                    if s == 0:
                        if routes(c):
                            router(n, 1)
                        recurrent(c, i)
                    if s == 2 and begins and c > 1:
                        pe.wait_ge(hpre_ready, c * J + 1)
                        if routes(c):
                            pe.wait_ge(z_ready, n + 1)
                        transpose_rows(c - 2)
                    if s == 5 and begins and c > 1:
                        pe.wait_ge(rows_ready, 2 * (c - 1))
                    if s == 5 and normalises(c, i):
                        transpose_x(n + 1, 1)
                    if s == 6 and routes(c):
                        pe.wait_ge(hpre_ready, i + (c * J + 1))
                        transpose_gates(n, 1)

            pe.wait_ge(const_landed, consts)
            transpose_x(0, J)
            router(0, J)
            for u in range(NS):
                if u == 0:
                    pe.wait_ge(wlo_ready, 1)
                first(0, 0, u)
            transpose_gates(0, J)
            transpose_x(1, 1)
            pe.wait_ge(wqlo_ready, 1)
            for c in range(NCH):
                for u in range(NS) if c > 0 else ():
                    first(c, 0, u)
                    second(c, 0, u - LAG)
                iterate(pe, c, iteration)
            for u in range(N - LAG, N):
                second(NCH - 1, 0, u)
            transpose_rows(NCH - 2)
            pe.wait_ge(rows_ready, 2 * (NCH - 1))
            transpose_rows(NCH - 1)

        @block.vector
        def _(dve):
            settled = partial(settle, dve)

            def row_stats(n, t, nj):
                for j in range(nj):
                    last = nc.vector.bn_stats(stats[:, j, :], xs[:, bass.ds(t + j, 1), :].squeeze(1))
                settled(last)
                for j in range(nj):
                    last = nc.vector.bn_aggr(mv[:, j, :], stats[:, j, :])
                settled(last)
                nc.vector.tensor_scalar(vare[:, 0:nj], mv[:, 0:nj, 1], 1e-5, None, ALU.add).then_inc(var_ready, 1)

            def normalise(n, t, nj):
                dve.wait_ge(rstd_ready, n + 1)
                if nj == 1:
                    dve.wait_ge(xt_ready, n)
                for j in range(nj):
                    last = nc.vector.tensor_scalar(xn[:, j, :], xs[:, bass.ds(t + j, 1), :].squeeze(1),
                                                   mv[:, j, 0:1], rstd[:, j:j + 1], ALU.subtract, ALU.mult)
                last.then_inc(xn_ready, 1)

            def low_x(n, t, nj):
                dve.wait_ge(xf_ready, n + 1)
                cols = bass.ds(t * P, nj * P)
                for kc, (dst, half) in enumerate(((bank_a, 0), (bank_b, 0)) if nj > 1 else ((bank_b, 0), (bank_b, 1))):
                    last = nc.vector.tensor_tensor(xlo[:, kc, cols], dst[:, half * P:half * P + nj * P],
                                                   xhi[:, kc, cols], ALU.subtract)
                last.then_inc(xlo_ready, 1)

            def add_bias(n, nj):
                dve.wait_ge(logits_ready, n + 1)
                nc.vector.tensor_tensor(zs[:, 0:nj, :], bank_b[:, 0:nj * E].rearrange("p (j e) -> p j e", j=nj),
                                        br_sb[:, :].unsqueeze(1).broadcast_to([P, nj, E]), ALU.add)\
                  .then_inc(z_ready, 1)

            def pick_groups(n, nj):
                dve.wait_ge(th_ready, n + 1)
                settled(nc.vector.tensor_scalar(ss[:, 0:nj, :], th[:, 0:nj, :], 0.5, 0.5, ALU.mult, ALU.add))
                s4 = ss[:, 0:nj, :].rearrange("p j (g e) -> p (j g) e", e=EG)
                pr = pairs[:, 0:nj * G, :]
                nc.vector.tensor_tensor(pr[:, :, 0:3], s4[:, :, 0:3], s4[:, :, 1:4], ALU.add)
                nc.vector.tensor_tensor(pr[:, :, 3:5], s4[:, :, 0:2], s4[:, :, 2:4], ALU.add)
                settled(nc.vector.tensor_tensor(pr[:, :, 5:6], s4[:, :, 0:1], s4[:, :, 3:4], ALU.add))
                settled(nc.vector.tensor_reduce(gsum[:, 0:nj, 0:G], pr.rearrange("p (j g) s -> p j g s", j=nj),
                                              AX.X, ALU.max))
                for j in range(nj):
                    last = nc.vector.max(top_g[:, j, :], gsum[:, j, 0:G])
                settled(last)
                settled(nc.vector.memset(top_g[:, 0:nj, KG:8], NONE))
                for j in range(nj):
                    last = nc.vector.match_replace(gmark[:, j, :], top_g[:, j, :], gsum[:, j, :], MARK)
                settled(last)
                settled(nc.vector.tensor_scalar(gmask[:, 0:nj, :], gmark[:, 0:nj, 0:G], MARK, None, ALU.is_ge))
                by_group = lambda a: a[:, 0:nj, 0:E].rearrange("p j (g e) -> p j g e", e=EG)
                settled(nc.vector.tensor_tensor(by_group(masked), by_group(ss),
                                              gmask[:, 0:nj, :].unsqueeze(3).broadcast_to([P, nj, G, EG]), ALU.mult))

            def pick_experts(n, nj):
                for j in range(nj):
                    last = nc.vector.max(top_e[:, j, :], masked[:, j, 0:E])
                settled(last)
                settled(nc.vector.memset(top_e[:, 0:nj, K:8], NONE))
                for j in range(nj):
                    last = nc.vector.match_replace(emark[:, j, :], top_e[:, j, :], masked[:, j, :], MARK)
                settled(last)
                settled(nc.vector.scalar_tensor_tensor(sel[:, 0:nj, :], emark[:, 0:nj, 0:E], MARK, ss[:, 0:nj, :],
                                                     ALU.is_ge, ALU.mult))
                settled(nc.vector.tensor_reduce(wsum[:, 0:nj], sel[:, 0:nj, :], AX.X, ALU.add))
                settled(nc.vector.tensor_scalar(wsum[:, 0:nj], wsum[:, 0:nj], 1e-20, None, ALU.add))
                settled(nc.vector.reciprocal(wrec[:, 0:nj], wsum[:, 0:nj]))
                if nj == 1:
                    dve.wait_ge(gt_ready, n)
                nc.vector.scalar_tensor_tensor(gate[:, 0:nj, :], sel[:, 0:nj, :], SCALE / W_SCALE ** 2,
                                               wrec[:, 0:nj].unsqueeze(2).broadcast_to([P, nj, E]),
                                               ALU.mult, ALU.mult).then_inc(gate_ready, 1)

            grouped = lambda a: a[:, :].rearrange("p (g w) -> p g w", w=GW)
            spread = lambda a: a[:, :].unsqueeze(2).broadcast_to([P, NG, GW])

            def rotate(c, i):
                t = i + c * J
                dve.wait_ge(q_ready, t + 1)
                q = bank_a[:, 0:D]
                at = i + c * J % (T // P)
                cs = cos_sb[:, bass.ds(at, 1), :].squeeze(1)
                sn = sin_sb[:, bass.ds(at, 1), :].squeeze(1)
                nc.vector.tensor_tensor(ra[:, :], q[:, 0:ROPE], cs, ALU.mult)
                by_pair = lambda a: a.rearrange("p (n two) -> p n two", two=2)
                nc.vector.tensor_tensor(by_pair(rb[:, :])[:, :, 0], by_pair(q[:, 0:ROPE])[:, :, 1],
                                        by_pair(sn)[:, :, 0], ALU.mult)
                settled(nc.vector.tensor_tensor(by_pair(rb[:, :])[:, :, 1], by_pair(q[:, 0:ROPE])[:, :, 0],
                                              by_pair(sn)[:, :, 1], ALU.mult))
                settled(nc.vector.tensor_tensor(ra[:, :], ra[:, :], rb[:, :], ALU.add))
                nc.vector.scalar_tensor_tensor(hpre[:, 0:ROPE], ra[:, :], 0.0, hbs[:, 0:ROPE], ALU.max, ALU.add)
                nc.vector.scalar_tensor_tensor(hpre[:, ROPE:D], q[:, ROPE:D], 0.0, hbs[:, ROPE:D],
                                               ALU.max, ALU.add).then_inc(hpre_ready, 1)

            def group_mean(t):
                dve.wait_ge(hh_ready, t + 1)
                settled(nc.vector.tensor_reduce(gmean[:, :], grouped(hh), AX.X, ALU.add))
                nc.vector.scalar_tensor_tensor(grouped(hd), spread(gmean), -1.0 / GW, grouped(hh), ALU.mult, ALU.add)\
                  .then_inc(hd_ready, 1)

            def group_var(t):
                dve.wait_ge(hsq_ready, t + 1)
                settled(nc.vector.tensor_reduce(gvar[:, :], grouped(hsq), AX.X, ALU.add))
                settled(nc.vector.tensor_scalar(gvare[:, :], gvar[:, :], 1.0 / GW, 1e-5, ALU.mult, ALU.add))
                settled(nc.vector.tensor_scalar(ghalf[:, :], gvare[:, :].bitcast(I32), 1, None,
                                              ALU.logical_shift_right))
                nc.vector.tensor_scalar(grstd[:, :].bitcast(I32), ghalf[:, :], -1.0, float(MAGIC),
                                        ALU.mult, ALU.add).then_inc(seed_ready, 1)

            def group_scale(c, i):
                t = i + c * J
                dve.wait_ge(grstd_ready, t + 1)
                if not (isinstance(t, int) and t == 0):
                    dve.wait_ge(hgain_ready, t)
                nc.vector.tensor_tensor(grouped(hnorm), grouped(hd), spread(grstd), ALU.mult)\
                  .then_inc(hnorm_ready, 1)

            def split_w(g, s):
                dve.wait_ge(whi_ready, g + 1)
                cols = bass.ds(g * WG, WG)
                nc.vector.scalar_tensor_tensor(wlo[:, cols], wst[:, s, :], W_SCALE, whi[:, cols],
                                               ALU.mult, ALU.subtract).then_inc(wlo_ready, 1)

            def half(k, s):
                dve.wait_ge(hi_done, k)
                nc.vector.tensor_tensor(hlo[:, s, :], hp[:, s, :], hhi[:, s, :], ALU.subtract)\
                  .then_inc(lo_done, 1)

            def step(c, i, u):
                k = c * N + u
                if k > 0:
                    half(i * BODY + k, slot(k - 1))
                if u < NS:
                    dve.wait_ge(relu_done, k + 1)
                else:
                    dve.wait_ge(gated, i * BODY + (c * E + u - NS + 1))
                s = slot(k)
                nc.vector.tensor_tensor(hp[:, s, :], relu[:, s, :], hp[:, s, :], ALU.mult).then_inc(h_done, 1)

            def finish_sum(c):
                for kc in range(KC):
                    dve.wait_ge(yth_ready, KC * c + kc + 1)
                    nc.vector.scalar_tensor_tensor(ysl[:, c % 2, kc, :], yth[:, kc, :], 1.0, acc[:, kc, :],
                                                   ALU.add, ALU.mult).then_inc(ysl_ready, 1)

            def mix(c):
                b, part = c // (NCH // B), c % (NCH // B)
                dve.wait_ge(ysl_ready, KC * (c + 1))
                dve.wait_ge(hn_ready, NT // B * (b + 1))
                tiles = hn[:, :, :].rearrange("p (b j k) d -> p b j k d", b=B, k=KC)
                for kc in range(KC):
                    branch = tiles[:, b, :, kc, part * P:(part + 1) * P].rearrange("p j q -> p q j")
                    y = ysl[:, c % 2, kc, :].rearrange("p (q j) -> p q j", j=J)
                    nc.vector.scalar_tensor_tensor(y, y, 0.5 / W_SCALE, branch, ALU.mult, ALU.mult)\
                      .then_inc(ymix_ready, 1)

            def finish_rows(c):
                for h, src in enumerate((bank_a, bank_b)):
                    dve.wait_ge(yt_ready, 2 * c + h + 1)
                    rows = xs[:, c * J + 2 * h:c * J + 2 * h + 2, :]
                    nc.vector.tensor_tensor(rows, src[:, :].rearrange("p (j d) -> p j d", j=2), rows, ALU.add)\
                      .then_inc(rows_ready, 1)

            def iteration(c, i):
                begins = isinstance(i, int) and i == 0
                n = i + (c * J + 1)
                t = i + c * J
                for s in range(BODY):
                    step(c, i, NS + s)
                    if s == 0 and begins and c > 0:
                        finish_sum(c - 1)
                    if s == 0 and routes(c):
                        add_bias(n, 1)
                    if s == 0 and normalises(c, i):
                        row_stats(n + 1, t + (J + 1), 1)
                    if s == 0:
                        rotate(c, i)
                    if s == 2 and normalises(c, i):
                        normalise(n + 1, t + (J + 1), 1)
                    if s == 2 and routes(c):
                        pick_groups(n, 1)
                    if s == 3:
                        group_mean(t)
                    if s == 3 and begins and c > 1:
                        finish_rows(c - 2)
                    if s == 4 and routes(c):
                        pick_experts(n, 1)
                    if s == 5:
                        group_var(t)
                    if s == 6 and normalises(c, i):
                        low_x(n + 1, t + (J + 1), 1)
                    if s == 7:
                        group_scale(c, i)
                    if s % 2 and c == 0 and not (isinstance(i, int) and i == ITERS - 1 and s > 1):
                        g = AHEAD + s // 2
                        split_w(i * (BODY // GROUP) + g, slot(g))

            nc.vector.memset(gsum[:, :, G:2 * G], NONE)
            settled(nc.vector.memset(masked[:, :, E:E + 8], NONE))
            dve.wait_ge(x_landed[0], 16)
            row_stats(0, 0, J)
            normalise(0, 0, J)
            low_x(0, 0, J)
            split_w(0, 0)
            dve.wait_ge(const_landed, consts)
            add_bias(0, J)
            pick_groups(0, J)
            pick_experts(0, J)
            nc.vector.tensor_scalar(hbs[:, :], hb_sb[:, :], WQ_SCALE, None, ALU.mult)
            dve.wait_ge(wqhi_ready, 1)
            nc.vector.scalar_tensor_tensor(wqlo[:, :, :], wq_sb[:, :, :], WQ_SCALE, wqhi[:, :, :],
                                           ALU.mult, ALU.subtract).then_inc(wqlo_ready, 1)
            split_w(1, 1)
            dve.wait_ge(x_landed[1], 16)
            row_stats(1, J, 1)
            normalise(1, J, 1)
            low_x(1, J, 1)
            for c in range(2, NCH):
                dve.wait_ge(x_landed[c], 16)
            for c in range(NCH):
                for u in range(NS):
                    step(c, 0, u)
                    if c == 0:
                        split_w(GROUP + u, GROUP + u)
                    if u == 0 and c > 1:
                        mix(c - 2)
                iterate(dve, c, iteration)
            half(NCH * N, slot(NCH * N - 1))
            mix(NCH - 2)
            finish_sum(NCH - 1)
            finish_rows(NCH - 2)
            mix(NCH - 1)
            finish_rows(NCH - 1)


def kernel(L0_attn_X, L0_attn_S_n, L0_attn_W_Q, L0_attn_hh_b, L0_attn_gn_weight, L0_attn_gn_bias,
           L0_ffn_Wr, L0_ffn_br, L0_ffn_W1, L0_ffn_W2, L0_ffn_Ws1, L0_ffn_Ws2):
    import concourse.bacc as bacc
    from concourse.bass_utils import run_bass_kernel_spmd

    arr = lambda a: np.asarray(a)
    flat = np.ascontiguousarray
    w1 = np.concatenate([arr(L0_ffn_Ws1).reshape(NS, M, D), arr(L0_ffn_W1)])
    w2 = np.concatenate([arr(L0_ffn_Ws2).reshape(D, NS, M).transpose(1, 0, 2), arr(L0_ffn_W2)])
    w1 = w1.reshape(N, M, KC, P).transpose(3, 0, 2, 1).reshape(P, N, D)
    w2 = w2.transpose(2, 0, 1)
    inv_freq = np.float32(1.0) / np.power(np.float32(10000.0), np.arange(0, ROPE, 2, dtype=np.float32) / np.float32(ROPE))
    angle = np.repeat(np.arange(T, dtype=np.float32)[:, None] * inv_freq.astype(np.float32)[None, :], 2, axis=1)
    by_tile = lambda a: flat(a.astype(np.float32).reshape(T // P, P, ROPE).transpose(1, 0, 2))
    sign = np.tile(np.array([-1.0, 1.0]), ROPE // 2)
    arrays = {
        "x": flat(arr(L0_attn_X).reshape(NCH, J, P, D)),
        "wts": flat(np.concatenate([w1, w2], axis=2).reshape(P, N * WCOLS)),
        "wr": flat(arr(L0_ffn_Wr).T.reshape(KC, P, E).transpose(1, 0, 2)),
        "br": arr(L0_ffn_br),
        "wq": flat(arr(L0_attn_W_Q).reshape(KC, P, D).transpose(1, 0, 2)),
        "hh_b": arr(L0_attn_hh_b),
        "gn_w": arr(L0_attn_gn_weight),
        "gn_b": arr(L0_attn_gn_bias),
        "cos": by_tile(np.cos(angle.astype(np.float64))),
        "sin": by_tile(np.sin(angle.astype(np.float64)) * sign),
        "ident": np.eye(P, dtype=np.float32),
    }
    nc = bacc.Bacc("TRN2", target_bir_lowering=False, num_devices=1)
    args = [nc.dram_tensor(f"in_{k}", a.shape, F32, kind="ExternalInput").ap() for k, a in arrays.items()]
    out = nc.dram_tensor("out", (NCH, J, P, D), F32, kind="ExternalOutput").ap()
    gates = nc.dram_tensor("gates", (NCH, E, CH), F32, kind="Internal").ap()
    build(nc, *args, out, gates)
    r = run_bass_kernel_spmd(nc, [{f"in_{k}": a for k, a in arrays.items()}], core_ids=[0])
    return r.results[0]["out"].reshape(B, T, D)
```

```python
import numpy as np
import concourse.bass as bass
from concourse import mybir
from contextlib import ExitStack
from functools import partial

ALU = mybir.AluOpType
ACT = mybir.ActivationFunctionType
AX = mybir.AxisListType
F32 = mybir.dt.float32
F16 = mybir.dt.float16
I32 = mybir.dt.int32

P = 128
B, T, D = 2, 1024, 256
KC = D // P
E, M = 32, 128
SH = 256
NS = SH // M
N = NS + E
G, EG = 8, E // 8
KG, K = 4, 6
CH = 512
NCH = B * T // CH
J = CH // P
NT = B * T // P
NG, GW = 32, 8
PAIR = 2
ROPE = 64
WCOLS = D + D
RING = 4
HRING = 8
BODY = 8
LAG = 4
EARLY = 6
AHEAD = 6
MAGIC = 0x5f3759df

W_SCALE = 64.0
WQ_SCALE = 256.0
WR_SCALE = 64.0
SCALE = 2.5
MARK = 4.0
NONE = -1.0


def build(nc, x, wts, wr, br, wq, hh_b, gn_w, gn_b, cos, sin, ident, out, gates):
    with ExitStack() as ctx:
        def sb(name, shape, dt=F32):
            return ctx.enter_context(nc.sbuf_tensor(name, shape, dt))

        def sem(name):
            return ctx.enter_context(nc.semaphore(name))

        xs = sb("xs", [P, NT, D])
        xh = sb("xh", [P, 2, KC, B * T], F16)
        xhi, xlo = xh[:, 0], xh[:, 1]
        whi = sb("whi", [P, N * WCOLS], F16)
        wlo = sb("wlo", [P, N * WCOLS], F16)
        hn = sb("hn", [P, NT, D])
        wr_sb = sb("wr_sb", [P, KC, E])
        wrhi = sb("wrhi", [P, KC, E], F16)
        wrlo = sb("wrlo", [P, KC, E], F16)
        br_sb = sb("br_sb", [1, E])
        brhi = sb("brhi", [1, E], F16)
        brlo = sb("brlo", [1, E], F16)
        ones = sb("ones", [1, P], F16)
        wq_sb = sb("wq_sb", [P, KC, D])
        wqhi = sb("wqhi", [P, KC, D], F16)
        wqlo = sb("wqlo", [P, KC, D], F16)
        hb_sb = sb("hb_sb", [P, D])
        hbs = sb("hbs", [P, D])
        gw_sb = sb("gw_sb", [P, D])
        gb_sb = sb("gb_sb", [P, D])
        cos_sb = sb("cos_sb", [P, T // P, ROPE])
        sin_sb = sb("sin_sb", [P, T // P, ROPE])
        id_sb = sb("id_sb", [P, P])
        id16 = sb("id16", [P, P], F16)
        power = sb("power", [P, J])
        wst = sb("wst", [P, RING, WCOLS])
        gate_bc = sb("gate_bc", [P, RING, CH])
        hid = sb("hid", [P, RING, CH])
        hhi = sb("hhi", [P, HRING, CH], F16)
        hlo = sb("hlo", [P, HRING, CH], F16)
        xn = sb("xn", [P, J, D])
        xn16 = sb("xn16", [P, 2, J, D], F16)
        stats = sb("stats", [P, J, 6])
        mv = sb("mv", [P, J, 2])
        vare = sb("vare", [P, J])
        rstd = sb("rstd", [P, J])
        nmean = sb("nmean", [P, J])
        shift = sb("shift", [P, J])
        th = sb("th", [P, J, E])
        ss = sb("ss", [P, J, E])
        pairs = sb("pairs", [P, J * G, 6])
        gsum = sb("gsum", [P, J, 2 * G])
        top_g = sb("top_g", [P, J, 8])
        gmark = sb("gmark", [P, J, 2 * G])
        gmask = sb("gmask", [P, J, G])
        masked = sb("masked", [P, J, E + 8])
        top_e = sb("top_e", [P, J, 8])
        emark = sb("emark", [P, J, E + 8])
        sel = sb("sel", [P, J, E])
        wsum = sb("wsum", [P, J])
        wrec = sb("wrec", [P, J])
        gate = sb("gate", [P, J, E])
        gate_t = sb("gate_t", [P, P])
        ra = sb("ra", [P, PAIR, ROPE])
        rb = sb("rb", [P, PAIR, ROPE])
        hpre = sb("hpre", [P, PAIR, D])
        hh = sb("hh", [P, PAIR, D])
        hd = sb("hd", [P, PAIR, D])
        hnorm = sb("hnorm", [P, PAIR, D])
        gmean = sb("gmean", [P, PAIR * NG])
        gvar = sb("gvar", [P, PAIR * NG])
        gvare = sb("gvare", [P, PAIR * NG])
        ghalf = sb("ghalf", [P, PAIR * NG], I32)
        grstd = sb("grstd", [P, PAIR * NG])
        gnewt = sb("gnewt", [P, PAIR * NG])
        yth = sb("yth", [P, KC, CH])
        ysl = sb("ysl", [P, 2, KC, CH])
        hp = ctx.enter_context(nc.psum_tensor("hp", [P, RING, CH], F32))
        acc = ctx.enter_context(nc.psum_tensor("acc", [P, KC, CH], F32))
        bank_a = ctx.enter_context(nc.psum_tensor("bank_a", [P, CH], F32))
        bank_b = ctx.enter_context(nc.psum_tensor("bank_b", [P, CH], F32))

        x_landed = [sem(f"x_landed{c}") for c in range(NCH)]
        x_rest_landed = sem("x_rest_landed")
        router_landed = sem("router_landed")
        branch_landed = sem("branch_landed")
        consts_ready = sem("consts_ready")
        w_landed = [sem(f"w_landed{s}") for s in range(RING)]
        gate_landed = [sem(f"gate_landed{s}") for s in range(RING)]
        gate_stored = sem("gate_stored")
        out_stored = sem("out_stored")
        var_ready = sem("var_ready")
        rstd_ready = sem("rstd_ready")
        xn_full_ready = sem("xn_full_ready")
        xn_hi_ready = sem("xn_hi_ready")
        xn_ready = sem("xn_ready")
        xt_ready = sem("xt_ready")
        xh_ready = sem("xh_ready")
        logits_ready = sem("logits_ready")
        th_ready = sem("th_ready")
        gate_ready = sem("gate_ready")
        gt_ready = sem("gt_ready")
        gts_ready = sem("gts_ready")
        wqhi_ready = sem("wqhi_ready")
        wqlo_ready = sem("wqlo_ready")
        q_ready = sem("q_ready")
        hpre_ready = sem("hpre_ready")
        hh_ready = sem("hh_ready")
        hd_ready = sem("hd_ready")
        hsq_ready = sem("hsq_ready")
        hnorm_ready = sem("hnorm_ready")
        seed_ready = sem("seed_ready")
        hn_ready = sem("hn_ready")
        whi_ready = sem("whi_ready")
        wlo_ready = sem("wlo_ready")
        l1_done = sem("l1_done")
        relu_done = sem("relu_done")
        square_done = sem("square_done")
        h_done = sem("h_done")
        hi_done = sem("hi_done")
        lo_done = sem("lo_done")
        acc_done = sem("acc_done")
        yth_ready = sem("yth_ready")
        ysl_ready = sem("ysl_ready")
        ymix_ready = sem("ymix_ready")
        yt_ready = sem("yt_ready")
        rows_ready = sem("rows_ready")

        router_consts, branch_consts = 16 * 3, 16 * 6
        ITERS = E // BODY
        BATCHES = NT - J + 1
        assert ITERS == J and BODY % RING == 0
        block = ctx.enter_context(nc.Block())

        def slot(k):
            return k % RING

        def looped(c):
            return 1, ITERS if c == 1 else ITERS - 1

        def routes(c):
            return c < NCH - 1

        def normalises(c, i):
            return c < NCH - 2 or (c == NCH - 2 and not (isinstance(i, int) and i == ITERS - 1))

        def branches(c):
            return 0 < c < NCH - 1

        def pair(c, i):
            return i + (c - 1) * ITERS

        def scales(c, i):
            first = isinstance(i, int) and i == 0
            return (branches(c) and not (c == 1 and first)) or (c == NCH - 1 and first)

        def splits(c, i, s):
            return c == 0 and not (isinstance(i, int) and i == ITERS - 1 and AHEAD + NS + i * BODY + s >= N)

        def iterate(engine, c, body):
            first, last = looped(c)
            body(c, 0)
            with engine.Fori(first, last) as i:
                body(c, i)
            for i in range(last, ITERS):
                body(c, i)

        def settle(engine, _):
            engine.drain()

        @block.sync
        def _(sp):
            def load_x(c):
                sp.dma_start(xs[:, c * J:(c + 1) * J, :], x[c].rearrange("j p d -> p j d"))\
                  .then_inc(x_landed[c], 16)

            def load_w(e, s):
                sp.dma_start(wst[:, s, :], wts[:, bass.ds(e * WCOLS, WCOLS)]).then_inc(w_landed[s], 16)

            for h, landed in enumerate((x_landed[0], x_rest_landed)):
                sp.dma_start(xs[:, 2 * h:2 * h + 2, :], x[0, 2 * h:2 * h + 2].rearrange("j p d -> p j d"))\
                  .then_inc(landed, 16)
            for dst, src in ((id_sb[:, :], ident), (wr_sb[:, :, :], wr), (br_sb[:, :], br)):
                sp.dma_start(dst, src).then_inc(router_landed, 16)
            load_w(0, 0)
            load_w(1, 1)
            load_x(1)
            for e in range(2, RING):
                load_w(e, e)
            for e in range(RING, AHEAD + NS):
                sp.wait_ge(wlo_ready, e - RING + 1)
                load_w(e, slot(e))
            for dst, src in ((wq_sb[:, :, :], wq), (hb_sb[:, :], hh_b.partition_broadcast(P)),
                             (gw_sb[:, :], gn_w.partition_broadcast(P)), (gb_sb[:, :], gn_b.partition_broadcast(P)),
                             (cos_sb[:, :, :], cos), (sin_sb[:, :, :], sin)):
                sp.dma_start(dst, src).then_inc(branch_landed, 16)
            for c in range(2, NCH):
                load_x(c)

            def load_gate(c, e, s):
                sp.dma_start(gate_bc[:, s, :], gates[c, bass.ds(e, 1), :].broadcast_to([P, CH]))\
                  .then_inc(gate_landed[s], 16)

            def iteration(c, i):
                for s in range(BODY):
                    if not (isinstance(i, int) and i == 0 and s < RING):
                        sp.wait_ge(h_done, i * BODY + (c * N + NS + s - RING + 1))
                    elif c > 0:
                        sp.wait_ge(h_done, c * N + s - RING + 1)
                    load_gate(c, i * BODY + s, slot(s))
                    if splits(c, i, s):
                        e = AHEAD + NS + s
                        sp.wait_ge(wlo_ready, i * BODY + (e - RING + 1))
                        load_w(i * BODY + e, slot(e))

            sp.wait_ge(gts_ready, 1)
            sp.dma_start(gates[0].rearrange("e (j p) -> j e p", p=P), gate_t[:, :]).then_inc(gate_stored, 16)
            for c in range(NCH):
                sp.wait_ge(gate_stored, 16 * (J * c + 1))
                iterate(sp, c, iteration)

        @block.gpsimd
        def _(pool):
            settled = partial(settle, pool)

            settled(nc.gpsimd.memset(power[:, :], -0.5))

            def row_rstd(n, nj):
                pool.wait_ge(var_ready, n + 1)
                root = nc.gpsimd.tensor_tensor(rstd[:, 0:nj], vare[:, 0:nj], power[:, 0:nj], ALU.pow)
                if isinstance(n, int) and n < 2:
                    root.then_inc(rstd_ready, 1)
                else:
                    settled(root)
                    nc.gpsimd.tensor_tensor(shift[:, 0:nj], nmean[:, 0:nj], rstd[:, 0:nj], ALU.mult)\
                      .then_inc(rstd_ready, 1)

            def low_x(t):
                pool.wait_ge(xn_hi_ready, t + 1)
                nc.gpsimd.tensor_tensor(xn16[:, 1, 0, :], xn[:, 0, :], xn16[:, 0, 0, :], ALU.subtract)\
                  .then_inc(xn_ready, 1)

            def newton():
                settled(nc.gpsimd.tensor_tensor(gnewt[:, :], grstd[:, :], grstd[:, :], ALU.mult))
                settled(nc.gpsimd.tensor_tensor(gnewt[:, :], gnewt[:, :], gvare[:, :], ALU.mult))
                settled(nc.gpsimd.tensor_scalar(gnewt[:, :], gnewt[:, :], -0.5, 1.5, ALU.mult, ALU.add))
                settled(nc.gpsimd.tensor_tensor(grstd[:, :], grstd[:, :], gnewt[:, :], ALU.mult))

            rows = lambda a: a[:, :].unsqueeze(1).broadcast_to([P, PAIR, D])

            def low(i, k):
                pool.wait_ge(hi_done, i * BODY + (k + 1))
                nc.gpsimd.tensor_tensor(hlo[:, k % HRING, :], hid[:, slot(k), :], hhi[:, k % HRING, :],
                                        ALU.subtract).then_inc(lo_done, 1)

            def iteration(c, i):
                q = pair(c, i)
                for s in range(BODY):
                    low(i, c * N + NS + s)
                    if scales(c, i):
                        if s == 0:
                            pool.wait_ge(seed_ready, q)
                            newton()
                        if s in (1, 2):
                            newton()
                        if s == 3:
                            by_group = hd[:, :, :].rearrange("p j (g w) -> p (j g) w", w=GW)
                            nc.gpsimd.tensor_tensor(hnorm[:, :, :].rearrange("p j (g w) -> p (j g) w", w=GW), by_group,
                                                    grstd[:, :].unsqueeze(2).broadcast_to([P, PAIR * NG, GW]),
                                                    ALU.mult).then_inc(hnorm_ready, 1)
                            pool.drain()
                        if s == 5:
                            settled(nc.gpsimd.tensor_tensor(hnorm[:, :, :], hnorm[:, :, :], rows(gw_sb), ALU.mult))
                        if s == 6:
                            nc.gpsimd.tensor_tensor(hn[:, bass.ds((q - 1) * PAIR, PAIR), :], hnorm[:, :, :],
                                                    rows(gb_sb), ALU.add).then_inc(hn_ready, 1)
                    if s == 0 and normalises(c, i):
                        row_rstd(i + (c * J + 2), 1)
                    if s == 1 and normalises(c, i):
                        low_x(i + ((c + 1) * J + 1))

            row_rstd(0, J)
            row_rstd(1, 1)
            for c in range(NCH):
                if c == 1:
                    pool.wait_ge(branch_landed, branch_consts)
                for u in range(NS):
                    low(0, c * N + u)
                iterate(pool, c, iteration)

        @block.scalar
        def _(act):
            def copy_x(t, src):
                act.wait_ge(xt_ready, t + 1)
                nc.scalar.activation(
                    xh[:, :, :, bass.ds(t * P, P)].rearrange("p h k t -> p (h k) t"),
                    src.bitcast(F16)[:, 0:2 * KC * P].rearrange("p (a t) -> p a t", t=P), ACT.Copy)\
                  .then_inc(xh_ready, 1)

            def tanh_z(n, nj):
                act.wait_ge(logits_ready, n + 1)
                nc.scalar.activation(th[:, 0:nj, :].rearrange("p j e -> p (j e)"), bank_b[:, 0:nj * E], ACT.Tanh,
                                     scale=0.5 / WR_SCALE).then_inc(th_ready, 1)

            def store_gates(n, c, j, nj):
                act.wait_ge(gt_ready, n + 1)
                if nj == 1:
                    act.wait_ge(gate_stored, n * 16)
                nc.scalar.activation(gate_t[0:nj * E, :], bank_a[0:nj * E, 0:P], ACT.Copy).then_inc(gts_ready, 1)
                if nj == 1:
                    act.wait_ge(gts_ready, n + 1)
                    act.dma_start(gates[c, :, bass.ds(j * P, P)], gate_t[0:E, :]).then_inc(gate_stored, 16)

            def high_x(t, j):
                act.wait_ge(xn_full_ready, t + 1)
                nc.scalar.activation(xn16[:, 0, j, :], xn[:, j, :], ACT.Copy).then_inc(xn_hi_ready, 1)

            def normalise(n, t):
                act.wait_ge(rstd_ready, n + 1)
                act.wait_ge(xt_ready, t)
                nc.scalar.activation(xn[:, 0, :], xs[:, bass.ds(t, 1), :].squeeze(1), ACT.Identity,
                                     scale=rstd[:, 0:1], bias=shift[:, 0:1]).then_inc(xn_full_ready, 1)
                high_x(t, 0)

            def split_w(e, s, landed):
                act.wait_ge(w_landed[s], landed)
                nc.scalar.activation(whi[:, bass.ds(e * WCOLS, WCOLS)], wst[:, s, :], ACT.Copy, scale=W_SCALE)\
                  .then_inc(whi_ready, 1)

            def half(i, k):
                act.wait_ge(h_done, i * BODY + (k + 1))
                nc.scalar.activation(hhi[:, k % HRING, :], hid[:, slot(k), :], ACT.Copy).then_inc(hi_done, 1)

            def step(c, i, u):
                k = c * N + u
                act.wait_ge(l1_done, i * BODY + (k + 1))
                if k >= RING or not (isinstance(i, int) and i == 0):
                    act.wait_ge(lo_done, i * BODY + (k - RING + 1))
                nc.scalar.activation(hid[:, slot(k), :], hp[:, slot(k), :], ACT.Relu).then_inc(relu_done, 1)
                act.wait_ge(relu_done, i * BODY + (k + 1))
                nc.scalar.activation(hid[:, slot(k), :], hid[:, slot(k), :], ACT.Square).then_inc(square_done, 1)
                if k > 0:
                    half(i, k - 1)

            def finish(c):
                for kc in range(KC):
                    act.wait_ge(acc_done, KC * c + kc + 1)
                    nc.scalar.activation(yth[:, kc, :], acc[:, kc, :], ACT.Tanh, scale=0.5 / W_SCALE)\
                      .then_inc(yth_ready, 1)

            def store(c):
                for h in range(2):
                    act.wait_ge(rows_ready, 2 * c + h + 1)
                    act.dma_start(out[c, 2 * h:2 * h + 2].rearrange("j p d -> p j d"),
                                  xs[:, c * J + 2 * h:c * J + 2 * h + 2, :]).then_inc(out_stored, 16)

            def iteration(c, i):
                q = pair(c, i)
                for s in range(BODY):
                    step(c, i, NS + s)
                    if s == LAG - 1 - NS and isinstance(i, int) and i == 0 and c > 0:
                        finish(c - 1)
                    if s == 0 and c == 0 and isinstance(i, int) and i == 0:
                        act.wait_ge(xt_ready, J)
                        high_x(J, 0)
                        copy_x(J, bank_b[:, :])
                    if s == 1 and routes(c):
                        tanh_z(i + (c * J + 1), 1)
                    if s == (2 if c == 0 else 1) and normalises(c, i):
                        normalise(i + (c * J + 2), i + ((c + 1) * J + 1))
                    if s == 4 and branches(c):
                        act.wait_ge(hpre_ready, q + 1)
                        nc.scalar.activation(hh[:, :, :], hpre[:, :, :], ACT.Tanh, scale=1.0 / WQ_SCALE)\
                          .then_inc(hh_ready, 1)
                    if s == 7 and normalises(c, i):
                        copy_x(i + ((c + 1) * J + 1), bank_b[:, :])
                    if s == 7 and routes(c):
                        store_gates(i + (c * J + 1), c + 1, i, 1)
                    if s == 6 and branches(c):
                        act.wait_ge(hd_ready, q + 1)
                        nc.scalar.activation(hh[:, :, :], hd[:, :, :], ACT.Square).then_inc(hsq_ready, 1)
                    for chunk, iter_, at in ((0, 0, 4), (1, 0, 7), (2, ITERS - 1, 4)):
                        if c == NCH - 1 and isinstance(i, int) and (i, s) == (iter_, at):
                            store(chunk)

            act.wait_ge(router_landed, router_consts)
            nc.scalar.activation(id16[:, :], id_sb[:, :], ACT.Copy)
            nc.scalar.activation(brhi[:, :], br_sb[:, :], ACT.Copy, scale=WR_SCALE)
            nc.scalar.activation(wrhi[:, :, :], wr_sb[:, :, :], ACT.Copy, scale=WR_SCALE).then_inc(consts_ready, 1)
            split_w(0, 0, 16)
            for j in range(J):
                high_x(j, j)
            split_w(1, 1, 16)
            for j in range(J):
                copy_x(j, hp[:, j, :])
            for e in range(2, RING):
                split_w(e, e, 16)
            tanh_z(0, J)
            for c in range(NCH):
                for u in range(NS):
                    step(c, 0, u)
                    if c == 0 and u == 0:
                        split_w(RING, 0, 32)
                        store_gates(0, 0, 0, J)
                        for e in range(RING + 1, AHEAD):
                            split_w(e, slot(e), 16 * (e // RING + 1))
                    if c == 0:
                        split_w(AHEAD + u, slot(AHEAD + u), 16 * ((AHEAD + u) // RING + 1))
                if c == 1:
                    act.wait_ge(branch_landed, branch_consts)
                    nc.scalar.activation(wqhi[:, :, :], wq_sb[:, :, :], ACT.Copy, scale=WQ_SCALE)\
                      .then_inc(wqhi_ready, 1)
                iterate(act, c, iteration)
            half(0, NCH * N - 1)
            finish(NCH - 1)
            store(NCH - 1)
            act.wait_ge(out_stored, 16 * 2 * NCH)

        @block.tensor
        def _(pe):
            def transpose_x(t, j, dst):
                pe.wait_ge(xn_ready, t + 1)
                for half in range(2):
                    for kc in range(KC):
                        at = (half * KC + kc) * P
                        mm = nc.tensor.transpose(dst.bitcast(F16)[:, at:at + P],
                                                 xn16[:, half, j, kc * P:(kc + 1) * P], id16[:, :])
                mm.then_inc(xt_ready, 1)

            def router(t, nj):
                for j in range(nj):
                    pe.wait_ge(xh_ready, t + (j + 1))
                    o = bank_b[:, j * E:(j + 1) * E]
                    cols = bass.ds((t + j) * P, P)
                    nc.tensor.matmul(o, ones[:, :], brhi[:, :], start=True, stop=False)
                    nc.tensor.matmul(o, ones[:, :], brlo[:, :], start=False, stop=False)
                    for kc in range(KC):
                        nc.tensor.matmul(o, xhi[:, kc, cols], wrlo[:, kc, :], start=False, stop=False)
                        nc.tensor.matmul(o, xlo[:, kc, cols], wrhi[:, kc, :], start=False, stop=False)
                        mm = nc.tensor.matmul(o, xhi[:, kc, cols], wrhi[:, kc, :], start=False, stop=(kc == KC - 1))
                mm.then_inc(logits_ready, 1)

            def transpose_gates(n, nj):
                pe.wait_ge(gate_ready, n + 1)
                if nj == 1:
                    pe.wait_ge(gts_ready, n)
                nc.tensor.transpose(bank_a[0:nj * E, 0:P], gate[:, 0:nj, :].rearrange("p j e -> p (j e)"),
                                    id_sb[:, :]).then_inc(gt_ready, 1)

            def queries(c, i):
                q = pair(c, i)
                pe.wait_ge(gts_ready, i + (c * J + 1))
                for j in range(PAIR):
                    o = bank_a[:, j * D:(j + 1) * D]
                    cols = bass.ds((q * PAIR + j) * P, P)
                    for kc in range(KC):
                        nc.tensor.matmul(o, xhi[:, kc, cols], wqhi[:, kc, :], start=(kc == 0), stop=False)
                        nc.tensor.matmul(o, xhi[:, kc, cols], wqlo[:, kc, :], start=False, stop=False)
                        mm = nc.tensor.matmul(o, xlo[:, kc, cols], wqhi[:, kc, :], start=False, stop=(kc == KC - 1))
                mm.then_inc(q_ready, 1)

            def first(c, i, u):
                k = c * N + u
                if k >= RING or not (isinstance(i, int) and i == 0):
                    pe.wait_ge(relu_done, i * BODY + (k - RING + 1))
                if c == 0:
                    pe.wait_ge(wlo_ready, i * BODY + (u + 1))
                cols = slice(c * CH, (c + 1) * CH)
                o = hp[:, slot(k), :]
                for kc in range(KC):
                    at = bass.ds(i * (BODY * WCOLS) + (u * WCOLS + kc * M), M)
                    nc.tensor.matmul(o, whi[:, at], xhi[:, kc, cols], start=(kc == 0), stop=False)
                    nc.tensor.matmul(o, whi[:, at], xlo[:, kc, cols], start=False, stop=False)
                    mm = nc.tensor.matmul(o, wlo[:, at], xhi[:, kc, cols], start=False, stop=(kc == KC - 1))
                mm.then_inc(l1_done, 1)

            def second(c, i, u):
                peeled = isinstance(i, int)
                if peeled and i == 0 and u < 0:
                    c, u = c - 1, u + N
                k = c * N + u
                pe.wait_ge(lo_done, i * BODY + (k + 1))
                begin, end = peeled and i == 0 and u == 0, peeled and u == N - 1
                for kc in range(KC):
                    if begin and c > 0:
                        pe.wait_ge(ysl_ready, KC * (c - 1) + kc + 1)
                    at = bass.ds(i * (BODY * WCOLS) + (u * WCOLS + D + kc * P), P)
                    o = acc[:, kc, :]
                    nc.tensor.matmul(o, whi[:, at], hhi[:, k % HRING, :], start=begin, stop=False, skip_group_check=True)
                    nc.tensor.matmul(o, whi[:, at], hlo[:, k % HRING, :], start=False, stop=False, skip_group_check=True)
                    mm = nc.tensor.matmul(o, wlo[:, at], hhi[:, k % HRING, :], start=False, stop=end,
                                          skip_group_check=True)
                    if end:
                        mm.then_inc(acc_done, 1)

            def transpose_rows(c):
                for kc in range(KC):
                    pe.wait_ge(ymix_ready, KC * c + kc + 1)
                    for h, dst in enumerate((bank_a, bank_b)):
                        for j in range(2):
                            at = (j * KC + kc) * P
                            tile = 2 * h + j
                            mm = nc.tensor.transpose(dst[:, at:at + P], ysl[:, c % 2, kc, tile * P:(tile + 1) * P],
                                                     id_sb[:, :])
                        if kc == KC - 1:
                            mm.then_inc(yt_ready, 1)

            def iteration(c, i):
                begins = isinstance(i, int) and i == 0
                n = i + (c * J + 1)
                for s in range(BODY):
                    u = NS + s
                    if not (c == 0 and begins and s < EARLY):
                        first(c, i, u)
                    if not (c == 0 and begins and u < LAG):
                        second(c, i, u - LAG)
                    if s == 0 and routes(c):
                        router(i + (c + 1) * J, 1)
                    if s == 1 and branches(c):
                        if c == 1 and begins:
                            pe.wait_ge(wqlo_ready, 1)
                        queries(c, i)
                    if s == 6 and normalises(c, i):
                        pe.wait_ge(th_ready, n + 1)
                        transpose_x(i + ((c + 1) * J + 1), 0, bank_b[:, :])
                    if s == 6 and routes(c):
                        if branches(c):
                            pe.wait_ge(hpre_ready, pair(c, i) + 1)
                        transpose_gates(n, 1)
                    for chunk, iter_, at in ((0, 0, 0), (1, 0, 5), (2, ITERS - 1, 0)):
                        if c == NCH - 1 and isinstance(i, int) and (i, s) == (iter_, at):
                            if chunk == 0:
                                pe.wait_ge(gts_ready, BATCHES)
                                pe.wait_ge(th_ready, BATCHES)
                            else:
                                pe.wait_ge(rows_ready, 2 * chunk)
                            transpose_rows(chunk)

            pe.wait_ge(consts_ready, 2)
            for j in range(J):
                transpose_x(j, j, hp[:, j, :])
            router(0, J)
            for u in range(NS + EARLY):
                first(0, 0, u)
                if u == NS:
                    transpose_gates(0, J)
                if u == NS + EARLY - 2:
                    pe.wait_ge(th_ready, 1)
                    transpose_x(J, 0, bank_b[:, :])
            for c in range(NCH):
                for u in range(NS) if c > 0 else ():
                    first(c, 0, u)
                    second(c, 0, u - LAG)
                iterate(pe, c, iteration)
            for u in range(N - LAG, N):
                second(NCH - 1, 0, u)
            pe.wait_ge(rows_ready, 2 * (NCH - 1))
            transpose_rows(NCH - 1)

        @block.vector
        def _(dve):
            settled = partial(settle, dve)

            def row_stats(n, t, nj):
                for j in range(nj):
                    if nj == J and j % 2 == 0:
                        dve.wait_ge(x_rest_landed if j else x_landed[0], 16)
                    last = nc.vector.bn_stats(stats[:, j, :], xs[:, bass.ds(t + j, 1), :].squeeze(1))
                settled(last)
                for j in range(nj):
                    last = nc.vector.bn_aggr(mv[:, j, :], stats[:, j, :])
                settled(last)
                nc.vector.tensor_scalar(nmean[:, 0:nj], mv[:, 0:nj, 0], -1.0, None, ALU.mult)
                nc.vector.tensor_scalar(vare[:, 0:nj], mv[:, 0:nj, 1], 1e-5, None, ALU.add).then_inc(var_ready, 1)

            def normalise(n, t, nj):
                dve.wait_ge(rstd_ready, n + 1)
                for j in range(nj):
                    nc.vector.tensor_scalar(xn[:, j, :], xs[:, t + j, :], mv[:, j, 0:1], rstd[:, j:j + 1],
                                            ALU.subtract, ALU.mult).then_inc(xn_full_ready, 1)
                for j in range(nj):
                    dve.wait_ge(xn_hi_ready, t + j + 1)
                    nc.vector.tensor_tensor(xn16[:, 1, j, :], xn[:, j, :], xn16[:, 0, j, :], ALU.subtract)\
                      .then_inc(xn_ready, 1)

            def pick_groups(n, nj):
                dve.wait_ge(th_ready, n + 1)
                settled(nc.vector.tensor_scalar(ss[:, 0:nj, :], th[:, 0:nj, :], 0.5, 0.5, ALU.mult, ALU.add))
                s4 = ss[:, 0:nj, :].rearrange("p j (g e) -> p (j g) e", e=EG)
                pr = pairs[:, 0:nj * G, :]
                nc.vector.tensor_tensor(pr[:, :, 0:3], s4[:, :, 0:3], s4[:, :, 1:4], ALU.add)
                nc.vector.tensor_tensor(pr[:, :, 3:5], s4[:, :, 0:2], s4[:, :, 2:4], ALU.add)
                settled(nc.vector.tensor_tensor(pr[:, :, 5:6], s4[:, :, 0:1], s4[:, :, 3:4], ALU.add))
                settled(nc.vector.tensor_reduce(gsum[:, 0:nj, 0:G], pr.rearrange("p (j g) s -> p j g s", j=nj),
                                              AX.X, ALU.max))
                for j in range(nj):
                    last = nc.vector.max(top_g[:, j, :], gsum[:, j, 0:G])
                settled(last)
                settled(nc.vector.memset(top_g[:, 0:nj, KG:8], NONE))
                for j in range(nj):
                    last = nc.vector.match_replace(gmark[:, j, :], top_g[:, j, :], gsum[:, j, :], MARK)
                settled(last)
                settled(nc.vector.tensor_scalar(gmask[:, 0:nj, :], gmark[:, 0:nj, 0:G], MARK, None, ALU.is_ge))
                by_group = lambda a: a[:, 0:nj, 0:E].rearrange("p j (g e) -> p j g e", e=EG)
                settled(nc.vector.tensor_tensor(by_group(masked), by_group(ss),
                                              gmask[:, 0:nj, :].unsqueeze(3).broadcast_to([P, nj, G, EG]), ALU.mult))

            def pick_experts(n, nj):
                for j in range(nj):
                    last = nc.vector.max(top_e[:, j, :], masked[:, j, 0:E])
                settled(last)
                settled(nc.vector.memset(top_e[:, 0:nj, K:8], NONE))
                for j in range(nj):
                    last = nc.vector.match_replace(emark[:, j, :], top_e[:, j, :], masked[:, j, :], MARK)
                settled(last)
                settled(nc.vector.scalar_tensor_tensor(sel[:, 0:nj, :], emark[:, 0:nj, 0:E], MARK, ss[:, 0:nj, :],
                                                     ALU.is_ge, ALU.mult))
                settled(nc.vector.tensor_reduce(wsum[:, 0:nj], sel[:, 0:nj, :], AX.X, ALU.add))
                settled(nc.vector.tensor_scalar(wsum[:, 0:nj], wsum[:, 0:nj], 1e-20, None, ALU.add))
                settled(nc.vector.reciprocal(wrec[:, 0:nj], wsum[:, 0:nj]))
                if nj == 1:
                    dve.wait_ge(gt_ready, n)
                nc.vector.scalar_tensor_tensor(gate[:, 0:nj, :], sel[:, 0:nj, :], SCALE / W_SCALE ** 2,
                                               wrec[:, 0:nj].unsqueeze(2).broadcast_to([P, nj, E]),
                                               ALU.mult, ALU.mult).then_inc(gate_ready, 1)

            grouped = lambda a: a[:, :, :].rearrange("p j (g w) -> p (j g) w", w=GW)

            def rotate(c, i):
                dve.wait_ge(q_ready, pair(c, i) + 1)
                q = bank_a[:, :].rearrange("p (j d) -> p j d", j=PAIR)
                cs = cos_sb[:, bass.ds(i * PAIR, PAIR), :]
                by_pair = lambda a: a.rearrange("p j (n two) -> p j n two", two=2)
                sn, rbp, qp = by_pair(sin_sb[:, bass.ds(i * PAIR, PAIR), :]), by_pair(rb[:, :, :]), by_pair(q[:, :, 0:ROPE])
                bias = lambda a, b: hbs[:, a:b].unsqueeze(1).broadcast_to([P, PAIR, b - a])
                nc.vector.tensor_tensor(ra[:, :, :], q[:, :, 0:ROPE], cs, ALU.mult)
                nc.vector.tensor_tensor(rbp[:, :, :, 0], qp[:, :, :, 1], sn[:, :, :, 0], ALU.mult)
                settled(nc.vector.tensor_tensor(rbp[:, :, :, 1], qp[:, :, :, 0], sn[:, :, :, 1], ALU.mult))
                settled(nc.vector.tensor_tensor(ra[:, :, :], ra[:, :, :], rb[:, :, :], ALU.add))
                nc.vector.scalar_tensor_tensor(hpre[:, :, 0:ROPE], ra[:, :, :], 0.0, bias(0, ROPE), ALU.max, ALU.add)
                nc.vector.scalar_tensor_tensor(hpre[:, :, ROPE:D], q[:, :, ROPE:D], 0.0, bias(ROPE, D),
                                               ALU.max, ALU.add).then_inc(hpre_ready, 1)

            def group_mean(c, i):
                dve.wait_ge(hh_ready, pair(c, i) + 1)
                settled(nc.vector.tensor_reduce(gmean[:, :], grouped(hh), AX.X, ALU.add))
                if scales(c, i):
                    dve.wait_ge(hnorm_ready, pair(c, i))
                nc.vector.scalar_tensor_tensor(grouped(hd), gmean[:, :].unsqueeze(2).broadcast_to([P, PAIR * NG, GW]),
                                               -1.0 / GW, grouped(hh), ALU.mult, ALU.add).then_inc(hd_ready, 1)

            def group_var(c, i):
                dve.wait_ge(hsq_ready, pair(c, i) + 1)
                settled(nc.vector.tensor_reduce(gvar[:, :], grouped(hh), AX.X, ALU.add))
                settled(nc.vector.tensor_scalar(gvare[:, :], gvar[:, :], 1.0 / GW, 1e-5, ALU.mult, ALU.add))
                settled(nc.vector.tensor_scalar(ghalf[:, :], gvare[:, :].bitcast(I32), 1, None,
                                              ALU.logical_shift_right))
                nc.vector.tensor_scalar(grstd[:, :].bitcast(I32), ghalf[:, :], -1.0, float(MAGIC),
                                        ALU.mult, ALU.add).then_inc(seed_ready, 1)

            def high_w(e, s, landed):
                dve.wait_ge(w_landed[s], landed)
                nc.vector.tensor_scalar(whi[:, bass.ds(e * WCOLS, WCOLS)], wst[:, s, :], W_SCALE, None, ALU.mult)

            def low_w(e, s):
                cols = bass.ds(e * WCOLS, WCOLS)
                nc.vector.scalar_tensor_tensor(wlo[:, cols], wst[:, s, :], W_SCALE, whi[:, cols],
                                               ALU.mult, ALU.subtract).then_inc(wlo_ready, 1)

            def split_w(e, s):
                dve.wait_ge(whi_ready, e + 1)
                low_w(e, s)

            def step(c, i, u):
                k = c * N + u
                if c > 0 and isinstance(i, int) and i == 0 and u == LAG - 1:
                    finish_sum(c - 1)
                dve.wait_ge(square_done, i * BODY + (k + 1))
                h = hid[:, slot(k), :]
                if u < NS:
                    nc.vector.tensor_scalar(h, h, 1.0 / W_SCALE ** 2, None, ALU.mult).then_inc(h_done, 1)
                else:
                    e = u - NS
                    dve.wait_ge(gate_landed[slot(e)], i * (16 * BODY // RING) + 16 * ((c * E + e) // RING + 1))
                    nc.vector.tensor_tensor(h, h, gate_bc[:, slot(e), :], ALU.mult).then_inc(h_done, 1)

            def finish_sum(c, kcs=range(KC)):
                if c > 1:
                    dve.wait_ge(yt_ready, 2 * (c - 1))
                for kc in kcs:
                    dve.wait_ge(yth_ready, KC * c + kc + 1)
                    nc.vector.scalar_tensor_tensor(ysl[:, c % 2, kc, :], yth[:, kc, :], 1.0, acc[:, kc, :],
                                                   ALU.add, ALU.mult).then_inc(ysl_ready, 1)

            def mix(c, kcs=range(KC)):
                b, part = c // (NCH // B), c % (NCH // B)
                dve.wait_ge(hn_ready, NT // B // PAIR * (b + 1))
                tiles = hn[:, :, :].rearrange("p (b j k) d -> p b j k d", b=B, k=KC)
                for kc in kcs:
                    dve.wait_ge(ysl_ready, KC * c + kc + 1)
                    branch = tiles[:, b, :, kc, part * P:(part + 1) * P].rearrange("p j q -> p q j")
                    y = ysl[:, c % 2, kc, :].rearrange("p (q j) -> p q j", j=J)
                    nc.vector.scalar_tensor_tensor(y, y, 0.5 / W_SCALE, branch, ALU.mult, ALU.mult)\
                      .then_inc(ymix_ready, 1)

            def finish_rows(c):
                for h, src in enumerate((bank_a, bank_b)):
                    dve.wait_ge(yt_ready, 2 * c + h + 1)
                    rows = xs[:, c * J + 2 * h:c * J + 2 * h + 2, :]
                    nc.vector.tensor_tensor(rows, src[:, :].rearrange("p (j d) -> p j d", j=2), rows, ALU.add)\
                      .then_inc(rows_ready, 1)

            def iteration(c, i):
                n = i + (c * J + 1)
                for s in range(BODY):
                    e = AHEAD + NS + s
                    step(c, i, NS + s)
                    if splits(c, i, s):
                        high_w(i * BODY + e, slot(e), i * (16 * BODY // RING) + 16 * (e // RING + 1))
                        dve.drain()
                        low_w(i * BODY + e, slot(e))
                    if s == 0 and normalises(c, i):
                        dve.wait_ge(xn_ready, n + J)
                        row_stats(n + 1, i + ((c + 1) * J + 1), 1)
                    if s == 1 and routes(c):
                        pick_groups(n, 1)
                    if s == 2 and routes(c):
                        pick_experts(n, 1)
                    if s == 3 and branches(c):
                        rotate(c, i)
                    if s == 5 and branches(c):
                        group_mean(c, i)
                    if s == 7 and branches(c):
                        group_var(c, i)
                    peeled = isinstance(i, int)
                    if c == NCH - 2 and peeled and (i, s) == (0, 7):
                        mix(0)
                    if c == NCH - 1 and peeled:
                        for chunk, iter_, at in ((1, 0, 3), (2, 0, 7)):
                            if (i, s) == (iter_, at):
                                mix(chunk)
                        for chunk, iter_, at in ((0, 0, 2), (1, 0, 6), (2, ITERS - 1, 1)):
                            if (i, s) == (iter_, at):
                                finish_rows(chunk)

            nc.vector.memset(gsum[:, :, G:2 * G], NONE)
            nc.vector.memset(ones[:, :], 1.0)
            nc.vector.memset(masked[:, :, E:E + 8], NONE)
            row_stats(0, 0, J)
            dve.wait_ge(consts_ready, 1)
            nc.vector.scalar_tensor_tensor(brlo[:, :], br_sb[:, :], WR_SCALE, brhi[:, :], ALU.mult, ALU.subtract)
            nc.vector.scalar_tensor_tensor(wrlo[:, :, :], wr_sb[:, :, :], WR_SCALE, wrhi[:, :, :],
                                           ALU.mult, ALU.subtract).then_inc(consts_ready, 1)
            normalise(0, 0, J)
            split_w(0, 0)
            split_w(1, 1)
            dve.wait_ge(x_landed[1], 16)
            row_stats(1, J, 1)
            split_w(2, 2)
            split_w(3, 3)
            pick_groups(0, J)
            pick_experts(0, J)
            for c in range(NCH):
                for u in range(NS):
                    step(c, 0, u)
                    if c == 0 and u == 0:
                        for e in range(RING, AHEAD):
                            split_w(e, slot(e))
                    if c == 0:
                        split_w(AHEAD + u, slot(AHEAD + u))
                if c == 0:
                    normalise(1, J, 1)
                if c == 1:
                    dve.wait_ge(wqhi_ready, 1)
                    nc.vector.tensor_scalar(hbs[:, :], hb_sb[:, :], WQ_SCALE, None, ALU.mult)
                    nc.vector.scalar_tensor_tensor(wqlo[:, :, :], wq_sb[:, :, :], WQ_SCALE, wqhi[:, :, :],
                                                   ALU.mult, ALU.subtract).then_inc(wqlo_ready, 1)
                if c + 2 < NCH:
                    dve.wait_ge(x_landed[c + 2], 16)
                iterate(dve, c, iteration)
            for kc in range(KC):
                finish_sum(NCH - 1, (kc,))
                mix(NCH - 1, (kc,))
            finish_rows(NCH - 1)


def kernel(L0_attn_X, L0_attn_S_n, L0_attn_W_Q, L0_attn_hh_b, L0_attn_gn_weight, L0_attn_gn_bias,
           L0_ffn_Wr, L0_ffn_br, L0_ffn_W1, L0_ffn_W2, L0_ffn_Ws1, L0_ffn_Ws2):
    import concourse.bacc as bacc
    from concourse.bass_utils import run_bass_kernel_spmd

    arr = lambda a: np.asarray(a)
    flat = np.ascontiguousarray
    w1 = np.concatenate([arr(L0_ffn_Ws1).reshape(NS, M, D), arr(L0_ffn_W1)])
    w2 = np.concatenate([arr(L0_ffn_Ws2).reshape(D, NS, M).transpose(1, 0, 2), arr(L0_ffn_W2)])
    w1 = w1.reshape(N, M, KC, P).transpose(3, 0, 2, 1).reshape(P, N, D)
    w2 = w2.transpose(2, 0, 1)
    inv_freq = np.float32(1.0) / np.power(np.float32(10000.0), np.arange(0, ROPE, 2, dtype=np.float32) / np.float32(ROPE))
    angle = np.repeat(np.arange(T, dtype=np.float32)[:, None] * inv_freq.astype(np.float32)[None, :], 2, axis=1)
    by_tile = lambda a: flat(a.astype(np.float32).reshape(T // P, P, ROPE).transpose(1, 0, 2))
    sign = np.tile(np.array([-1.0, 1.0]), ROPE // 2)
    arrays = {
        "x": flat(arr(L0_attn_X).reshape(NCH, J, P, D)),
        "wts": flat(np.concatenate([w1, w2], axis=2).reshape(P, N * WCOLS)),
        "wr": flat(arr(L0_ffn_Wr).T.reshape(KC, P, E).transpose(1, 0, 2)),
        "br": arr(L0_ffn_br).reshape(1, E),
        "wq": flat(arr(L0_attn_W_Q).reshape(KC, P, D).transpose(1, 0, 2)),
        "hh_b": arr(L0_attn_hh_b),
        "gn_w": arr(L0_attn_gn_weight),
        "gn_b": arr(L0_attn_gn_bias),
        "cos": by_tile(np.cos(angle.astype(np.float64))),
        "sin": by_tile(np.sin(angle.astype(np.float64)) * sign),
        "ident": np.eye(P, dtype=np.float32),
    }
    nc = bacc.Bacc("TRN2", target_bir_lowering=False, num_devices=1)
    args = [nc.dram_tensor(f"in_{k}", a.shape, F32, kind="ExternalInput").ap() for k, a in arrays.items()]
    out = nc.dram_tensor("out", (NCH, J, P, D), F32, kind="ExternalOutput").ap()
    gates = nc.dram_tensor("gates", (NCH, E, CH), F32, kind="Internal").ap()
    build(nc, *args, out, gates)
    r = run_bass_kernel_spmd(nc, [{f"in_{k}": a for k, a in arrays.items()}], core_ids=[0])
    return r.results[0]["out"].reshape(B, T, D)
```
